# Optimizing a Trainium2 kernel written in Bass

```python
import numpy as np
import jax
import jax.numpy as jnp

def _softmax(x, axis=-1):
    return jax.nn.softmax(x, axis=axis)

def _gelu(x):
    return jax.nn.gelu(x, approximate=True)

def _silu(x):
    return jax.nn.silu(x)

def _sigmoid(x):
    return jax.nn.sigmoid(x)

def _layernorm(x, axis=-1, eps=1e-05):
    m = jnp.mean(x, axis=axis, keepdims=True)
    v = jnp.var(x, axis=axis, keepdims=True)
    return (x - m) / jnp.sqrt(v + eps)

def _scatter_add(tgt, idx, src, axis=0):
    return tgt.at[idx].add(src)

def _segment_sum(src, seg, n):
    return jax.ops.segment_sum(src, seg, n)
kernel_name = 'mk_decoder_preln_d2_seqx_r4_8380a1'

def setup_inputs(seed: int=0):
    np.random.seed(seed)
    _w = jnp.asarray

    def _rec_inputs():
        import jax
        import jax.numpy as jnp
        _rk = jax.random.key(seed)
        x = -0.0002928 + 1 * jax.random.normal(jax.random.fold_in(_rk, 1), (64, 128, 256), jnp.float32)
        _lenS = 128 - jax.random.randint(jax.random.fold_in(_rk, 7), (64,), 0, max(1, 128 // 4) + 1, jnp.int32)
        _lenS2 = 128 - jax.random.randint(jax.random.fold_in(_rk, 8), (64,), 0, max(1, 128 // 4) + 1, jnp.int32)
        _ctx_1024P = jax.random.normal(jax.random.fold_in(_rk, 11), (64, 16, 256), jnp.float32)
        _ctx_1024c = jax.random.dirichlet(jax.random.fold_in(_rk, 511), 0.3 * jnp.ones((16,), jnp.float32), (64, 128))
        _ctx_1024t = jnp.einsum('bsk,bkd->bsd', _ctx_1024c, _ctx_1024P)
        _ctx_1024t = _ctx_1024t * jax.lax.rsqrt(jnp.mean(jnp.square(_ctx_1024t)) + 1e-12) * 0.953939
        ctx_1024 = -1.39393e-06 + 0.999914 * (_ctx_1024t + 0.3 * jax.random.normal(jax.random.fold_in(_rk, 611), (64, 128, 256), jnp.float32))
        return (x, ctx_1024)
    x, ctx_1024 = _rec_inputs()

    def _L0_attn_setup():
        import jax, jax.numpy as jnp
        import numpy as np
        from jax.scipy.linalg import solve_triangular
        B, T, D = (2, 1024, 256)
        HEAD_DIM = 128
        CHUNK = 64

        def _forward(out, W_write, W_read, W_alpha, W_beta, A_log, dt_bias):
            Bs, Ts, Ds = out.shape
            d, C = (HEAD_DIM, CHUNK)
            H = Ds // d
            x = out.astype(jnp.float32)
            rk = x.reshape(Bs, Ts, H, d)
            rk = rk / jnp.maximum(jnp.linalg.norm(rk, axis=-1, keepdims=True), 1e-12)
            rk = jnp.swapaxes(rk, 1, 2)
            wk = jnp.pad(rk[:, :, :-1], ((0, 0), (0, 0), (1, 0), (0, 0)))
            v = jnp.einsum('btd,ed->bte', x, W_write).reshape(Bs, Ts, H, d)
            v = jnp.swapaxes(v, 1, 2)
            beta = jax.nn.sigmoid(jnp.einsum('btd,hd->bth', x, W_beta))
            beta = jnp.swapaxes(beta, 1, 2)[..., None]
            log_decay = -jnp.exp(A_log)[None, None, :] * jax.nn.softplus(jnp.einsum('btd,hd->bth', x, W_alpha) + dt_bias)
            log_decay = jnp.swapaxes(log_decay, 1, 2)
            v_scaled = v * beta
            wk_scaled = wk * beta
            pad = -Ts % C
            if pad:
                p4 = ((0, 0), (0, 0), (0, pad), (0, 0))
                rk = jnp.pad(rk, p4)
                wk = jnp.pad(wk, p4)
                v_scaled = jnp.pad(v_scaled, p4)
                wk_scaled = jnp.pad(wk_scaled, p4)
                log_decay = jnp.pad(log_decay, ((0, 0), (0, 0), (0, pad)))
            Tp = Ts + pad
            N = Tp // C
            chunk = lambda a: a.reshape(Bs, H, N, C, d)
            rk, wk, v_scaled, wk_scaled = map(chunk, (rk, wk, v_scaled, wk_scaled))
            log_decay = log_decay.reshape(Bs, H, N, C)
            cum = jnp.cumsum(log_decay, -1)
            L_mask = jnp.tril(jnp.exp(jnp.tril(cum[..., :, None] - cum[..., None, :])))
            decay_exp = jnp.exp(cum)[..., None]
            chunk_end_decay = jnp.exp(cum[..., -1])
            M = jnp.tril(-(wk_scaled @ jnp.swapaxes(wk, -1, -2)) * L_mask, -1)
            eye = jnp.eye(C, dtype=x.dtype)
            A = solve_triangular(eye - M, jnp.broadcast_to(eye, M.shape), lower=True, unit_diagonal=True)
            intra = jnp.tril(rk @ jnp.swapaxes(wk, -1, -2) * L_mask, -1)
            rk_decay = rk * decay_exp
            tail_decay = jnp.exp(cum[..., -1:] - cum)[..., None]
            wk_pos = jnp.swapaxes(wk * tail_decay, -1, -2)
            wk_scaled_dec = wk_scaled * decay_exp
            toN = lambda a: jnp.moveaxis(a, 2, 0)

            def step(S, inp):
                A_i, vsc_i, wkd_i, rkd_i, intra_i, wkp_i, ced_i = inp
                v_new = A_i @ vsc_i - A_i @ wkd_i @ S
                o_i = rkd_i @ S + intra_i @ v_new
                S = ced_i[..., None, None] * S + wkp_i @ v_new
                return (S, o_i)
            S0 = jnp.zeros((Bs, H, d, d), x.dtype)
            _, o = jax.lax.scan(step, S0, (toN(A), toN(v_scaled), toN(wk_scaled_dec), toN(rk_decay), toN(intra), toN(wk_pos), jnp.moveaxis(chunk_end_decay, 2, 0)))
            o = jnp.moveaxis(o, 0, 2).reshape(Bs, H, Tp, d)
            o = jnp.swapaxes(o, 1, 2).reshape(Bs, Tp, Ds)[:, :Ts]
            return out + jnp.einsum('btd,ed->bte', o, W_read).astype(out.dtype)
        key = jax.random.key(seed)
        ks = jax.random.split(key, 7)
        H = D // HEAD_DIM
        out = jax.random.normal(ks[0], (B, T, D), dtype=jnp.float32)
        scale = D ** (-0.5)
        W_write = jax.random.normal(ks[1], (D, D), jnp.float32) * scale
        W_read = jax.random.normal(ks[2], (D, D), jnp.float32) * scale
        W_alpha = jax.random.normal(ks[3], (H, D), jnp.float32) * scale
        W_beta = jax.random.normal(ks[4], (H, D), jnp.float32) * scale
        A_log = jnp.log(jax.random.uniform(ks[5], (H,), jnp.float32, 0.05, 16.0))
        dt_bias = jnp.ones((H,), jnp.float32)
        return {'out': out, 'W_write': W_write, 'W_read': W_read, 'W_alpha': W_alpha, 'W_beta': W_beta, 'A_log': A_log, 'dt_bias': dt_bias}
    _L0_attn_all = _L0_attn_setup()
    _L0_attn_in = {k: v for k, v in _L0_attn_all.items() if k in ('W_write', 'W_read', 'W_alpha', 'W_beta', 'A_log', 'dt_bias')}
    del _L0_attn_all

    def _L0_xattn_setup():
        import jax, jax.numpy as jnp
        import numpy as np
        B, S, D, H = (2, 512, 256, 16)
        DK = D // H

        def _quantum(x, W1, b1, W2, b2):
            return jnp.tanh(x @ W1 + b1) @ W2 + b2
        key = jax.random.key(seed)
        ks = jax.random.split(key, 16)
        s = 1.0 / np.sqrt(DK)
        inp = {'q': jax.random.normal(ks[0], (B, S, D), dtype=jnp.float32), 'k': jax.random.normal(ks[1], (B, S, D), dtype=jnp.float32), 'v': jax.random.normal(ks[2], (B, S, D), dtype=jnp.float32)}
        names = ['q', 'k', 'v']
        for i, n in enumerate(names):
            inp[f'W{n}1'] = jax.random.normal(ks[3 + 4 * i], (DK, DK), dtype=jnp.float32) * s
            inp[f'b{n}1'] = jnp.zeros((DK,), dtype=jnp.float32)
            inp[f'W{n}2'] = jax.random.normal(ks[4 + 4 * i], (DK, DK), dtype=jnp.float32) * s
            inp[f'b{n}2'] = jnp.zeros((DK,), dtype=jnp.float32)
        inp['Wo'] = jax.random.normal(ks[15], (D, D), dtype=jnp.float32) * (1.0 / np.sqrt(D))
        inp['bo'] = jnp.zeros((D,), dtype=jnp.float32)
        return inp
    _L0_xattn_all = _L0_xattn_setup()
    _L0_xattn_in = {k: v for k, v in _L0_xattn_all.items() if k in ('Wq1', 'bq1', 'Wq2', 'bq2', 'Wk1', 'bk1', 'Wk2', 'bk2', 'Wv1', 'bv1', 'Wv2', 'bv2', 'Wo', 'bo')}
    del _L0_xattn_all

    def _L0_ffn_setup():
        import jax, jax.numpy as jnp
        import numpy as np
        EPS_LN = 1e-05
        EPS_GATE = 1e-08

        def layer_norm(x, gamma, beta):
            mu = jnp.mean(x, axis=-1, keepdims=True)
            var = jnp.mean(jnp.square(x - mu), axis=-1, keepdims=True)
            return (x - mu) * jax.lax.rsqrt(var + EPS_LN) * gamma + beta
        key = jax.random.key(seed)
        ks = jax.random.split(key, 8)
        B, S, D, E, H = (4, 1024, 256, 4, 512)
        s_in = 1.0 / np.sqrt(D)
        s_h = 1.0 / np.sqrt(H)
        return {'h': jax.random.normal(ks[0], (B, S, D), dtype=jnp.float32), 'router_w': jax.random.uniform(ks[1], (E, D), jnp.float32, -s_in, s_in), 'rn_g': jnp.ones((D,), jnp.float32), 'rn_b': jnp.zeros((D,), jnp.float32), 'w1': jax.random.uniform(ks[2], (E, D, H), jnp.float32, -s_in, s_in), 'ln_g': jnp.ones((E, H), jnp.float32), 'ln_b': jnp.zeros((E, H), jnp.float32), 'w2': jax.random.uniform(ks[3], (E, H, D), jnp.float32, -s_h, s_h), 'on_g': jnp.ones((D,), jnp.float32), 'on_b': jnp.zeros((D,), jnp.float32)}
    _L0_ffn_all = _L0_ffn_setup()
    _L0_ffn_in = {k: v for k, v in _L0_ffn_all.items() if k in ('router_w', 'rn_g', 'rn_b', 'w1', 'ln_g', 'ln_b', 'w2', 'on_g', 'on_b')}
    del _L0_ffn_all

    def _L1_attn_setup():
        import jax, jax.numpy as jnp
        import numpy as np
        N_EMBD = 256
        N_HEAD = 16
        HEAD_DIM = N_EMBD // N_HEAD
        LATENT_DIM = N_EMBD // 2
        B, T = (4, 512)
        key = jax.random.key(seed)
        ks = jax.random.split(key, 5)

        def init(k, fan_in, fan_out):
            bound = 1.0 / np.sqrt(fan_in)
            return jax.random.uniform(k, (fan_in, fan_out), jnp.float32, -bound, bound)
        return {'x': jax.random.normal(ks[0], (B, T, N_EMBD), jnp.float32), 'Wc_down': init(ks[1], N_EMBD, LATENT_DIM), 'Wq_up': init(ks[2], LATENT_DIM, N_EMBD), 'Wkv_up': init(ks[3], LATENT_DIM, 2 * HEAD_DIM), 'Wc_proj': init(ks[4], N_EMBD, N_EMBD)}
    _L1_attn_all = _L1_attn_setup()
    _L1_attn_in = {k: v for k, v in _L1_attn_all.items() if k in ('Wc_down', 'Wq_up', 'Wkv_up', 'Wc_proj')}
    del _L1_attn_all

    def _L1_xattn_setup():
        import jax, jax.numpy as jnp
        import numpy as np
        import math
        DIM = 256
        N_HEADS = 16
        HEAD_DIM = DIM // N_HEADS
        BATCH = 4
        SEQ = 512
        key = jax.random.key(seed)
        ks = jax.random.split(key, 7)
        scale = 1.0 / math.sqrt(DIM)
        return {'q': jax.random.normal(ks[0], (BATCH, SEQ, DIM), jnp.float32), 'k': jax.random.normal(ks[1], (BATCH, SEQ, DIM), jnp.float32), 'v': jax.random.normal(ks[2], (BATCH, SEQ, DIM), jnp.float32), 'wq': jax.random.normal(ks[3], (DIM, DIM), jnp.float32) * scale, 'wk': jax.random.normal(ks[4], (DIM, DIM), jnp.float32) * scale, 'wv': jax.random.normal(ks[5], (DIM, DIM), jnp.float32) * scale, 'wo': jax.random.normal(ks[6], (DIM, DIM), jnp.float32) * scale}
    _L1_xattn_all = _L1_xattn_setup()
    _L1_xattn_in = {k: v for k, v in _L1_xattn_all.items() if k in ('wq', 'wk', 'wv', 'wo')}
    del _L1_xattn_all

    def _L1_ffn_setup():
        import jax, jax.numpy as jnp
        import numpy as np
        NUM_EXPERTS = 8
        TOP_K = 2
        D_MODEL = 256
        EXPERT_CAP = 128
        B, S = (4, 512)
        key = jax.random.key(seed)
        ks = jax.random.split(key, 4)
        scale = 1.0 / np.sqrt(D_MODEL)
        x = jax.random.normal(ks[0], (B, S, D_MODEL), dtype=jnp.float32)
        gate_w = jax.random.normal(ks[1], (D_MODEL, NUM_EXPERTS), dtype=jnp.float32) * scale
        w1 = jax.random.normal(ks[2], (NUM_EXPERTS, D_MODEL, EXPERT_CAP), dtype=jnp.float32) * scale
        b1 = jnp.zeros((NUM_EXPERTS, EXPERT_CAP), dtype=jnp.float32)
        w2 = jax.random.normal(ks[3], (NUM_EXPERTS, EXPERT_CAP, D_MODEL), dtype=jnp.float32) * (1.0 / np.sqrt(EXPERT_CAP))
        b2 = jnp.zeros((NUM_EXPERTS, D_MODEL), dtype=jnp.float32)
        return {'x': x, 'gate_w': gate_w, 'w1': w1, 'b1': b1, 'w2': w2, 'b2': b2}
    _L1_ffn_all = _L1_ffn_setup()
    _L1_ffn_in = {k: v for k, v in _L1_ffn_all.items() if k in ('gate_w', 'w1', 'b1', 'w2', 'b2')}
    del _L1_ffn_all
    return {'x': x, 'ctx_1024': ctx_1024, 'L0_attn_W_write': _L0_attn_in['W_write'], 'L0_attn_W_read': _L0_attn_in['W_read'], 'L0_attn_W_alpha': _L0_attn_in['W_alpha'], 'L0_attn_W_beta': _L0_attn_in['W_beta'], 'L0_attn_A_log': _L0_attn_in['A_log'], 'L0_attn_dt_bias': _L0_attn_in['dt_bias'], 'L0_xattn_Wq1': _L0_xattn_in['Wq1'], 'L0_xattn_bq1': _L0_xattn_in['bq1'], 'L0_xattn_Wq2': _L0_xattn_in['Wq2'], 'L0_xattn_bq2': _L0_xattn_in['bq2'], 'L0_xattn_Wk1': _L0_xattn_in['Wk1'], 'L0_xattn_bk1': _L0_xattn_in['bk1'], 'L0_xattn_Wk2': _L0_xattn_in['Wk2'], 'L0_xattn_bk2': _L0_xattn_in['bk2'], 'L0_xattn_Wv1': _L0_xattn_in['Wv1'], 'L0_xattn_bv1': _L0_xattn_in['bv1'], 'L0_xattn_Wv2': _L0_xattn_in['Wv2'], 'L0_xattn_bv2': _L0_xattn_in['bv2'], 'L0_xattn_Wo': _L0_xattn_in['Wo'], 'L0_xattn_bo': _L0_xattn_in['bo'], 'L0_ffn_router_w': _L0_ffn_in['router_w'], 'L0_ffn_rn_g': _L0_ffn_in['rn_g'], 'L0_ffn_rn_b': _L0_ffn_in['rn_b'], 'L0_ffn_w1': _L0_ffn_in['w1'], 'L0_ffn_ln_g': _L0_ffn_in['ln_g'], 'L0_ffn_ln_b': _L0_ffn_in['ln_b'], 'L0_ffn_w2': _L0_ffn_in['w2'], 'L0_ffn_on_g': _L0_ffn_in['on_g'], 'L0_ffn_on_b': _L0_ffn_in['on_b'], 'L1_attn_Wc_down': _L1_attn_in['Wc_down'], 'L1_attn_Wq_up': _L1_attn_in['Wq_up'], 'L1_attn_Wkv_up': _L1_attn_in['Wkv_up'], 'L1_attn_Wc_proj': _L1_attn_in['Wc_proj'], 'L1_xattn_wq': _L1_xattn_in['wq'], 'L1_xattn_wk': _L1_xattn_in['wk'], 'L1_xattn_wv': _L1_xattn_in['wv'], 'L1_xattn_wo': _L1_xattn_in['wo'], 'L1_ffn_gate_w': _L1_ffn_in['gate_w'], 'L1_ffn_w1': _L1_ffn_in['w1'], 'L1_ffn_b1': _L1_ffn_in['b1'], 'L1_ffn_w2': _L1_ffn_in['w2'], 'L1_ffn_b2': _L1_ffn_in['b2']}

def reference(x, ctx_1024, L0_attn_W_write, L0_attn_W_read, L0_attn_W_alpha, L0_attn_W_beta, L0_attn_A_log, L0_attn_dt_bias, L0_xattn_Wq1, L0_xattn_bq1, L0_xattn_Wq2, L0_xattn_bq2, L0_xattn_Wk1, L0_xattn_bk1, L0_xattn_Wk2, L0_xattn_bk2, L0_xattn_Wv1, L0_xattn_bv1, L0_xattn_Wv2, L0_xattn_bv2, L0_xattn_Wo, L0_xattn_bo, L0_ffn_router_w, L0_ffn_rn_g, L0_ffn_rn_b, L0_ffn_w1, L0_ffn_ln_g, L0_ffn_ln_b, L0_ffn_w2, L0_ffn_on_g, L0_ffn_on_b, L1_attn_Wc_down, L1_attn_Wq_up, L1_attn_Wkv_up, L1_attn_Wc_proj, L1_xattn_wq, L1_xattn_wk, L1_xattn_wv, L1_xattn_wo, L1_ffn_gate_w, L1_ffn_w1, L1_ffn_b1, L1_ffn_w2, L1_ffn_b2):
    import jax
    import jax.numpy as jnp

    def _L0_attn_ref(out, W_write, W_read, W_alpha, W_beta, A_log, dt_bias):
        import jax, jax.numpy as jnp
        import numpy as np
        from jax.scipy.linalg import solve_triangular
        B, T, D = (2, 1024, 256)
        HEAD_DIM = 128
        CHUNK = 64

        def _forward(out, W_write, W_read, W_alpha, W_beta, A_log, dt_bias):
            Bs, Ts, Ds = out.shape
            d, C = (HEAD_DIM, CHUNK)
            H = Ds // d
            x = out.astype(jnp.float32)
            rk = x.reshape(Bs, Ts, H, d)
            rk = rk / jnp.maximum(jnp.linalg.norm(rk, axis=-1, keepdims=True), 1e-12)
            rk = jnp.swapaxes(rk, 1, 2)
            wk = jnp.pad(rk[:, :, :-1], ((0, 0), (0, 0), (1, 0), (0, 0)))
            v = jnp.einsum('btd,ed->bte', x, W_write).reshape(Bs, Ts, H, d)
            v = jnp.swapaxes(v, 1, 2)
            beta = jax.nn.sigmoid(jnp.einsum('btd,hd->bth', x, W_beta))
            beta = jnp.swapaxes(beta, 1, 2)[..., None]
            log_decay = -jnp.exp(A_log)[None, None, :] * jax.nn.softplus(jnp.einsum('btd,hd->bth', x, W_alpha) + dt_bias)
            log_decay = jnp.swapaxes(log_decay, 1, 2)
            v_scaled = v * beta
            wk_scaled = wk * beta
            pad = -Ts % C
            if pad:
                p4 = ((0, 0), (0, 0), (0, pad), (0, 0))
                rk = jnp.pad(rk, p4)
                wk = jnp.pad(wk, p4)
                v_scaled = jnp.pad(v_scaled, p4)
                wk_scaled = jnp.pad(wk_scaled, p4)
                log_decay = jnp.pad(log_decay, ((0, 0), (0, 0), (0, pad)))
            Tp = Ts + pad
            N = Tp // C
            chunk = lambda a: a.reshape(Bs, H, N, C, d)
            rk, wk, v_scaled, wk_scaled = map(chunk, (rk, wk, v_scaled, wk_scaled))
            log_decay = log_decay.reshape(Bs, H, N, C)
            cum = jnp.cumsum(log_decay, -1)
            L_mask = jnp.tril(jnp.exp(jnp.tril(cum[..., :, None] - cum[..., None, :])))
            decay_exp = jnp.exp(cum)[..., None]
            chunk_end_decay = jnp.exp(cum[..., -1])
            M = jnp.tril(-(wk_scaled @ jnp.swapaxes(wk, -1, -2)) * L_mask, -1)
            eye = jnp.eye(C, dtype=x.dtype)
            A = solve_triangular(eye - M, jnp.broadcast_to(eye, M.shape), lower=True, unit_diagonal=True)
            intra = jnp.tril(rk @ jnp.swapaxes(wk, -1, -2) * L_mask, -1)
            rk_decay = rk * decay_exp
            tail_decay = jnp.exp(cum[..., -1:] - cum)[..., None]
            wk_pos = jnp.swapaxes(wk * tail_decay, -1, -2)
            wk_scaled_dec = wk_scaled * decay_exp
            toN = lambda a: jnp.moveaxis(a, 2, 0)

            def step(S, inp):
                A_i, vsc_i, wkd_i, rkd_i, intra_i, wkp_i, ced_i = inp
                v_new = A_i @ vsc_i - A_i @ wkd_i @ S
                o_i = rkd_i @ S + intra_i @ v_new
                S = ced_i[..., None, None] * S + wkp_i @ v_new
                return (S, o_i)
            S0 = jnp.zeros((Bs, H, d, d), x.dtype)
            _, o = jax.lax.scan(step, S0, (toN(A), toN(v_scaled), toN(wk_scaled_dec), toN(rk_decay), toN(intra), toN(wk_pos), jnp.moveaxis(chunk_end_decay, 2, 0)))
            o = jnp.moveaxis(o, 0, 2).reshape(Bs, H, Tp, d)
            o = jnp.swapaxes(o, 1, 2).reshape(Bs, Tp, Ds)[:, :Ts]
            return out + jnp.einsum('btd,ed->bte', o, W_read).astype(out.dtype)
        return _forward(out, W_write, W_read, W_alpha, W_beta, A_log, dt_bias)

    def _L0_xattn_ref(q, k, v, Wq1, bq1, Wq2, bq2, Wk1, bk1, Wk2, bk2, Wv1, bv1, Wv2, bv2, Wo, bo):
        import jax, jax.numpy as jnp
        import numpy as np
        B, S, D, H = (2, 512, 256, 16)
        DK = D // H

        def _quantum(x, W1, b1, W2, b2):
            return jnp.tanh(x @ W1 + b1) @ W2 + b2
        b, s, _ = q.shape
        qh = q.reshape(b, s, H, DK)
        kh = k.reshape(b, s, H, DK)
        vh = v.reshape(b, s, H, DK)
        qh = _quantum(qh, Wq1, bq1, Wq2, bq2)
        kh = _quantum(kh, Wk1, bk1, Wk2, bk2)
        vh = _quantum(vh, Wv1, bv1, Wv2, bv2)
        scale = 1.0 / jnp.sqrt(jnp.asarray(DK, dtype=qh.dtype))
        scores = jnp.einsum('bqhd,bkhd->bhqk', qh, kh) * scale
        attn = jax.nn.softmax(scores, axis=-1)
        ctx = jnp.einsum('bhqk,bkhd->bqhd', attn, vh).reshape(b, s, D)
        return ctx @ Wo + bo

    def _L0_ffn_ref(h, router_w, rn_g, rn_b, w1, ln_g, ln_b, w2, on_g, on_b):
        import jax, jax.numpy as jnp
        import numpy as np
        EPS_LN = 1e-05
        EPS_GATE = 1e-08

        def layer_norm(x, gamma, beta):
            mu = jnp.mean(x, axis=-1, keepdims=True)
            var = jnp.mean(jnp.square(x - mu), axis=-1, keepdims=True)
            return (x - mu) * jax.lax.rsqrt(var + EPS_LN) * gamma + beta
        D = h.shape[-1]
        h_norm = layer_norm(h, rn_g, rn_b)
        g = jax.nn.softmax(jnp.einsum('bsd,ed->bse', h_norm, router_w), axis=-1)
        top2_w, top2_idx = jax.lax.top_k(g, 2)
        top2_w = top2_w / (jnp.sum(top2_w, axis=-1, keepdims=True) + EPS_GATE)
        hid = jnp.einsum('bsd,edh->bseh', h, w1)
        hid = jax.nn.relu(layer_norm(hid, ln_g, ln_b))
        expert_out = jnp.einsum('bseh,ehd->bsed', hid, w2)
        idx = jnp.broadcast_to(top2_idx[..., None], top2_idx.shape + (D,))
        top2_out = jnp.take_along_axis(expert_out, idx, axis=-2)
        out = jnp.sum(top2_out * top2_w[..., None], axis=-2)
        return layer_norm(out, on_g, on_b)

    def _L1_attn_ref(x, Wc_down, Wq_up, Wkv_up, Wc_proj):
        import jax, jax.numpy as jnp
        import numpy as np
        N_EMBD = 256
        N_HEAD = 16
        HEAD_DIM = N_EMBD // N_HEAD
        LATENT_DIM = N_EMBD // 2
        B, T = (4, 512)
        Bsz, Tlen, C = x.shape
        latent = x @ Wc_down
        q = (latent @ Wq_up).reshape(Bsz, Tlen, N_HEAD, HEAD_DIM)
        kv = latent @ Wkv_up
        k, v = (kv[..., :HEAD_DIM], kv[..., HEAD_DIM:])
        scale = 1.0 / np.sqrt(HEAD_DIM)
        att = jnp.einsum('bthd,bsd->bhts', q, k) * scale
        causal = jnp.tril(jnp.ones((Tlen, Tlen), dtype=bool))
        att = jnp.where(causal[None, None], att, -jnp.inf)
        att = jax.nn.softmax(att, axis=-1)
        y = jnp.einsum('bhts,bsd->bthd', att, v).reshape(Bsz, Tlen, C)
        return y @ Wc_proj

    def _L1_xattn_ref(q, k, v, wq, wk, wv, wo):
        import jax, jax.numpy as jnp
        import numpy as np
        import math
        DIM = 256
        N_HEADS = 16
        HEAD_DIM = DIM // N_HEADS
        BATCH = 4
        SEQ = 512
        bsz, seqlen, _ = q.shape

        def proj(x, w):
            return (x @ w).reshape(bsz, seqlen, N_HEADS, HEAD_DIM).transpose(0, 2, 1, 3)
        xq, xk, xv = (proj(q, wq), proj(k, wk), proj(v, wv))
        scores = jnp.einsum('bhqd,bhkd->bhqk', xq, xk) / math.sqrt(HEAD_DIM)
        causal = jnp.triu(jnp.full((seqlen, seqlen), -jnp.inf, jnp.float32), k=1)
        scores = scores + causal[None, None, :, :]
        attn = jax.nn.softmax(scores.astype(jnp.float32), axis=-1).astype(xq.dtype)
        out = jnp.einsum('bhqk,bhkd->bhqd', attn, xv)
        out = out.transpose(0, 2, 1, 3).reshape(bsz, seqlen, -1)
        return out @ wo

    def _L1_ffn_ref(x, gate_w, w1, b1, w2, b2):
        import jax, jax.numpy as jnp
        import numpy as np
        NUM_EXPERTS = 8
        TOP_K = 2
        D_MODEL = 256
        EXPERT_CAP = 128
        B, S = (4, 512)
        Bx, Sx, D = x.shape
        xt = x.reshape(-1, D)
        gates = jax.nn.softmax(xt @ gate_w, axis=-1)
        topk_g, topk_i = jax.lax.top_k(gates, TOP_K)
        tok_w = topk_g.sum(axis=-1)
        sel = (topk_i[:, :, None] == jnp.arange(NUM_EXPERTS)[None, None, :]).any(axis=1)
        h = jax.nn.gelu(jnp.einsum('nd,edh->enh', xt, w1) + b1[:, None, :], approximate=False)
        y = jnp.einsum('enh,ehd->end', h, w2) + b2[:, None, :]
        out = jnp.einsum('end,ne,n->nd', y, sel.astype(x.dtype), tok_w)
        return out.reshape(Bx, Sx, D)
    x = x + _L0_attn_ref(_layernorm(x, axis=-1), L0_attn_W_write, L0_attn_W_read, L0_attn_W_alpha, L0_attn_W_beta, L0_attn_A_log, L0_attn_dt_bias)
    x = x + _L0_xattn_ref(_layernorm(x, axis=-1), ctx_1024, ctx_1024, L0_xattn_Wq1, L0_xattn_bq1, L0_xattn_Wq2, L0_xattn_bq2, L0_xattn_Wk1, L0_xattn_bk1, L0_xattn_Wk2, L0_xattn_bk2, L0_xattn_Wv1, L0_xattn_bv1, L0_xattn_Wv2, L0_xattn_bv2, L0_xattn_Wo, L0_xattn_bo)
    x = x + _L0_ffn_ref(_layernorm(x, axis=-1), L0_ffn_router_w, L0_ffn_rn_g, L0_ffn_rn_b, L0_ffn_w1, L0_ffn_ln_g, L0_ffn_ln_b, L0_ffn_w2, L0_ffn_on_g, L0_ffn_on_b)
    x = x + _L1_attn_ref(_layernorm(x, axis=-1), L1_attn_Wc_down, L1_attn_Wq_up, L1_attn_Wkv_up, L1_attn_Wc_proj)
    x = x + _L1_xattn_ref(_layernorm(x, axis=-1), ctx_1024, ctx_1024, L1_xattn_wq, L1_xattn_wk, L1_xattn_wv, L1_xattn_wo)
    x = x + _L1_ffn_ref(_layernorm(x, axis=-1), L1_ffn_gate_w, L1_ffn_w1, L1_ffn_b1, L1_ffn_w2, L1_ffn_b2)
    return x

_drawn_inputs = setup_inputs


def setup_inputs(seed=0):
    import zlib

    import numpy as np

    out = dict(_drawn_inputs(seed))
    spreads = {'L0_attn_dt_bias': (1.0, 0.6),
     'L0_xattn_bq1': (0.0, 0.579),
     'L0_xattn_bq2': (0.0, 0.556),
     'L0_xattn_bk1': (0.0, 0.8),
     'L0_xattn_bk2': (0.0, 0.8),
     'L0_xattn_bv1': (0.0, 0.1),
     'L0_xattn_bv2': (0.0, 0.1),
     'L0_xattn_bo': (0.0, 0.1),
     'L0_ffn_rn_g': (1.0, 0.2),
     'L0_ffn_rn_b': (0.0, 0.1),
     'L0_ffn_ln_g': (1.0, 0.2),
     'L0_ffn_ln_b': (0.0, 0.1),
     'L0_ffn_on_g': (1.0, 0.2),
     'L0_ffn_on_b': (0.0, 0.1),
     'L1_ffn_b1': (0.0, 0.335),
     'L1_ffn_b2': (0.0, 0.1)}
    factors = {'L0_attn_W_write': 8.0,
     'L0_attn_W_read': 8.0,
     'L0_attn_W_alpha': 8.0,
     'L0_attn_W_beta': 8.0,
     'L0_attn_A_log': 8.0,
     'L1_attn_Wq_up': 7.301}
    for name, (base, spread) in spreads.items():
        noise = np.random.default_rng([zlib.crc32(name.encode()), seed]).standard_normal(out[name].shape)
        drawn = base * np.exp(spread * noise) if base else spread * noise
        out[name] = jnp.asarray(drawn.astype(out[name].dtype))
    for name, factor in factors.items():
        out[name] = (out[name] * factor).astype(out[name].dtype)
    return out
```

```python
from contextlib import ExitStack

import concourse.bass as bass
from concourse import mybir

ALU = mybir.AluOpType
ACT = mybir.ActivationFunctionType
F32 = mybir.dt.float32
BF16 = mybir.dt.bfloat16
AX = mybir.AxisListType.X

P = 128
D = 256
C = D // P
G = 4
N = G * P
NH = 16
HD = D // NH
QH = 4
QUADS = G * NH // QH
HPC = P // HD
DH = 2
CHUNK = 64
PB = 8
PG = 2
LANES = 4
UNROLL = 3
RUN = 16
E0, H0 = 4, 512
KC0 = H0 // P
E1, H1 = 8, 128
LEVELS = 7
LN_EPS = 1e-5
MASKED = -1e30
SCALE = HD ** -0.5

PER = dict(
    ln_stats=4 * 8, ln_parts=3 * 8, ln_mean=2 * 8, ln_var=8, ln_log=8, ln_rstd=8, ln_fix=5 * 8, xn=4 * 6, xT_psum=2 * 6, xT_act=6, xT_dve=6,
    ctx_psum=2, ctxT_act=1, ctxT_dve=1, rk_sq=8, rk_max=1, rk_log=1, rk_rs=1, rk=1, rk_psum=2,
    rkT_act=1, rkT_dve=1, ab_psum=1, beta_exp=1,
    beta_1p=1, beta=1, col_psum=1, col=1, row_psum=2, dec_neg=1,
    dec_off=2, dec_diff=2, dec_min=1, dec_exp=1, dec_strict=1, dec_beta=2, G_psum=2, R_psum=2,
    MT=2, IT=2, V_psum=2, Vb=2, lev=14, inv_eye=2, W_psum=12, W=12, U_psum=12, U=12,
    T_psum=12, T=12, vnew_psum=2, vnew=2, oT_psum=2, oT=2, y0_psum=2,
    h_psum=6, h_act=6, lat_psum=1, lat=1, q_psum=6, q=6, k_psum=5, k=5, km=20, v_psum=5, v=6,
    s_psum=48, s_max=48, s_sub=48, p_exp=48, t_psum=48, pt=48, pv=48, o_sb=12, otr_psum=12,
    o_rec=12, o_norm=12, attT_psum=12, attT=12, y_psum=6,
    res=10, bias_res=3, xin_used=1,
    r_psum=1, r_fix=3, g_max=2, g_sub=2, g_exp=2, g_sum=2, g_rec=2, g_prob=2,
    g_cmp=2, g_lt=2, g_cmp2=2, g_ge=2, g_cnt=2, g_rank=2, g_sel=2, g_top=2, g_tsum=2, g_trec=1, g_w=2,
    up_psum=16, up_stats=16, up_parts=12, up_mean=8, up_var=4, up_log=4, up_rstd=4, up_fix=5 * 4, z=16, zT_psum=16, zT=16, dn_psum=8, acc=16,
    moe_g=4,
    gl_psum=1, gT_psum=1, gT=1, h1_psum=8, h1=8, b2_psum=2, y1_psum=16, acc1=34,
)


def decoder_kernel(nc, a, out):
    NB = a["x"].shape[0]
    NIT = NB // G
    NPG = NB // (PB * PG)
    R = NB * DH
    x_r = a["x"].rearrange("(q b) t d -> q t b d", b=PB)
    x_d = a["x"].rearrange("(i b) t d -> i t b d", b=G)
    ctx_d = a["ctx_1024"].rearrange("(i b) t d -> i t b d", b=G)
    out_d = out.rearrange("(i b) t d -> i t b d", b=G)

    with ExitStack() as ctx:
        def sb(name, shape, dt=F32):
            return ctx.enter_context(nc.sbuf_tensor(name, shape, dt))

        def sem(name):
            return ctx.enter_context(nc.semaphore(name))

        ident = sb("ident", [P, P])
        identb = sb("identb", [P, P], BF16)
        strict = sb("strict", [P, P])
        levmask = sb("levmask", [P, LEVELS, P])
        causal = sb("causal", [P, QH, P], BF16)
        headmask = sb("headmask", [P, HPC])
        rep16 = sb("rep16", [HD, HPC, HD])
        rowsel = sb("rowsel", [DH, DH, P])
        lo = sb("lo", [P, 1])
        ones = sb("ones", [P, P])
        lt_mask = sb("lt_mask", [P, E1, E1])
        ge_mask = sb("ge_mask", [P, E1, E1])
        colcum = sb("colcum", [P, NB * DH])
        eps_ln = sb("eps_ln", [P, 1])
        ln_shift = sb("ln_shift", [P, 1])

        resets = sb("resets", [R, P])
        run_resets = sb("run_resets", [R, P // RUN])

        WwT = sb("WwT", [P, C, D])
        WrT = sb("WrT", [P, C, D])
        Wab = sb("Wab", [P, C, DH])
        a_col = sb("a_col", [R, 2])
        qw_raw = sb("qw_raw", [HD, 6 * HD + 6])
        Wblk = sb("Wblk", [P, 6, HPC, HD])
        bcol = sb("bcol", [P, 6])
        bv2_row = sb("bv2_row", [P, HD])
        Wo0 = sb("Wo0", [P, C, D])
        bo_row = sb("bo_row", [P, D])
        rwT = sb("rwT", [P, C, E0])
        rn_g = sb("rn_g", [P, C])
        rn_b = sb("rn_b", [P, C])
        rgb = sb("rgb", [P, C, 2, E0])
        rsum = sb("rsum", [P, 2, E0])
        w1_0 = sb("w1_0", [P, E0, C, H0])
        w2_0 = sb("w2_0", [P, E0, KC0, D])
        lng = sb("lng", [P, E0, KC0])
        lnb = sb("lnb", [P, E0, KC0])
        ong_row = sb("ong_row", [P, D])
        onb_row = sb("onb_row", [P, D])
        Wcd = sb("Wcd", [P, C, P])
        Wqu = sb("Wqu", [P, D])
        Wkv = sb("Wkv", [P, 2 * HD])
        Wkr = sb("Wkr", [P, HPC, HD])
        Wcp = sb("Wcp", [P, C, D])
        wq = sb("wq", [P, C, D])
        wk = sb("wk", [P, C, D])
        wv = sb("wv", [P, C, D])
        wo = sb("wo", [P, C, D])
        gw = sb("gw", [P, C, E1])
        w1_1 = sb("w1_1", [P, E1, C, H1])
        b1_1 = sb("b1_1", [H1, E1])
        w2_1 = sb("w2_1", [H1, E1, D])
        b2_1 = sb("b2_1", [E1, D])

        arena = sb("arena", [P, 26 * G * D])

        def cut(first, *shape):
            size = 1
            for n in shape:
                size *= n
            flat = arena[:, first * G * D:first * G * D + size]
            names = "abcde"[:len(shape)]
            return flat.rearrange(f"p ({' '.join(names)}) -> p {' '.join(names)}", **dict(zip(names, shape)))

        x_in = cut(13, G, D)
        ctx_in = cut(14, G, D)
        xres = cut(15, G, D)
        xn = cut(16, G, D)
        xT = cut(17, C, N)
        ctxT = cut(18, C, N)
        stats = sb("stats", [P, G, 6])
        parts = sb("parts", [P, 4, G])
        mv = sb("mv", [P, G, 2])
        lnv = sb("lnv", [P, G])
        rstd = sb("rstd", [P, G])
        w_nat = cut(4, 2, C, D)
        same = cut(5, LEVELS + 1, P)
        ssq = sb("ssq", [P, G * DH])
        rnl = sb("rnl", [P, G * DH])
        rns = sb("rns", [P, G * DH])
        rk = cut(0, G * DH, P)
        rkT = sb("rkT", [P, DH, G, P + 1])
        bet = sb("bet", [DH, N])
        crow = cut(24, G, DH, P)
        col = sb("col", [P, G, DH])
        off = sb("off", [P, DH, G, 2])
        dec = cut(1, DH, N)
        decb = cut(2, DH, N)
        MT = cut(3, DH, N)
        IT = cut(4, DH, N)
        lev = cut(5, 2, DH, N)
        Tm = cut(7, DH, N)
        Um = cut(8, DH, N)
        Wm = cut(9, DH, N)
        Vb = cut(10, G, D)
        vnew = cut(11, DH, N)
        oT = cut(12, DH, N)
        hT = cut(4, 3, C, N)
        latT = sb("latT", [P, N])
        QT = cut(8, C, N)
        KT = cut(7, C, N)
        KM = cut(0, 2, C, HPC, P)
        V2 = cut(19, G, NH, 2 * HD)
        smax = sb("smax", [P, QUADS, QH])
        Ssb = cut(21, 4, QH, P)
        PT = cut(11, 2, QH, P)
        osb = cut(10, 2, N)
        orec = sb("orec", [P, G, NH])
        att = cut(12, 2, NH, HD)
        attT = cut(9, C, N)
        r_raw = sb("r_raw", [P, G, E1])
        r_lg = sb("r_lg", [P, G, E1])
        gmx = sb("gmx", [P, G])
        gsm = sb("gsm", [P, G])
        grc = sb("grc", [P, G])
        gp = sb("gp", [P, G, E1])
        cmp1 = cut(25, G, E1, E1)
        cmp2 = cut(23, G, E1, E1)
        rank = sb("rank", [P, G, E1])
        gsel = sb("gsel", [P, G, E1])
        gtop = sb("gtop", [P, G, E1])
        gate = sb("gate", [P, G, E1])
        ust = sb("ust", [P, 4, 6])
        uparts = sb("uparts", [P, 4, G])
        umv = sb("umv", [P, 4, 2])
        ulg = sb("ulg", [P, 4])
        urs = sb("urs", [P, 4])
        z = cut(4, 2, G, H0)
        zT = cut(8, 2, KC0, N)
        acc = cut(0, G, D)
        gT = arena[0:E1, 12 * G * D + N:13 * G * D]
        h1 = cut(4, E1, N)

        rx, rh, rl, rt = (cut(2 * n, PB, D) for n in range(4))
        rp, re = (cut(n, PG, DH, PB, D) for n in (8, 16))
        dw = cut(24, 3, DH, D)
        small = arena[:, 25 * G * D + G * D // 2:26 * G * D]
        lan = small[:, 0:PB * RUN].rearrange("p (b n) -> p b n", n=RUN)
        lan2 = small[:, PB * RUN:PB * RUN + PB * 8].rearrange("p (b n) -> p b n", n=8)
        row = small[:, PB * RUN + PB * 8:PB * RUN + PB * 28].rearrange("p (n b) -> p n b", b=PB)
        acc_s, acc_a, acc_b, acc_c, acc_d = (arena[:, 2048 + 128 * n:2048 + 128 * (n + 1)].rearrange("p (n l) -> p n l", l=LANES) for n in range(5))
        au = sb("au", [P, R])
        dec_t = [arena[0:R, 8192 + 256 * n:8192 + 256 * n + P + 1] for n in range(20)]
        cum_all = sb("cum_all", [R, P])
        run_sum = sb("run_sum", [R, P // RUN + 1])
        run_pre = sb("run_pre", [R, P // RUN])
        cum_dram = nc.dram_tensor("cum_dram", (R, P), F32, kind="Internal").ap()

        bank = [ctx.enter_context(nc.psum_tensor(f"bank{n}", [P, 512], F32)) for n in range(8)]

        S = {name: sem(name) for name in PER}
        loaded_x, loaded_c, stored = sem("loaded_x"), sem("loaded_c"), sem("stored")
        w_loaded, set_pool, set_pe, set_dve = (sem(n) for n in ("w_loaded", "set_pool", "set_pe", "set_dve"))

        loaded_r, ref_step, ref_x, ref_var, ref_seed, decay_step, au_psum, cum_psum, cum_ready, cum_stored, loaded_row = (
            sem(n) for n in ("loaded_r", "ref_step", "ref_x", "ref_var", "ref_seed", "decay_step", "au_psum", "cum_psum", "cum_ready", "cum_stored", "loaded_row"))
        v_ones = sem("v_ones")

        def at(it, name, n):
            assert n > 0
            return it * PER[name] + n

        block = ctx.enter_context(nc.Block())
        heads = lambda t: t.rearrange("p (g t) -> p g t", t=P)

        loads = [
            (w_nat[:, 0], a["L0_attn_W_write"].rearrange("(c p) d -> p c d", p=P)),
            (w_nat[:, 1], a["L0_attn_W_read"].rearrange("(c p) d -> p c d", p=P)),
            (Wo0[:, :, :], a["L0_xattn_Wo"].rearrange("(c p) d -> p c d", p=P)),
            (bv2_row[:, :], a["L0_xattn_bv2"].partition_broadcast(P)),
            (bo_row[:, :], a["L0_xattn_bo"].partition_broadcast(P)),
            (ong_row[:, :], a["L0_ffn_on_g"].partition_broadcast(P)),
            (onb_row[:, :], a["L0_ffn_on_b"].partition_broadcast(P)),
            (rn_g[:, :], a["L0_ffn_rn_g"].rearrange("(c p) -> p c", p=P)),
            (rn_b[:, :], a["L0_ffn_rn_b"].rearrange("(c p) -> p c", p=P)),
            (Wcd[:, :, :], a["L1_attn_Wc_down"].rearrange("(c p) d -> p c d", p=P)),
            (Wqu[:, :], a["L1_attn_Wq_up"]),
            (Wkv[:, :], a["L1_attn_Wkv_up"]),
            (Wcp[:, :, :], a["L1_attn_Wc_proj"].rearrange("(c p) d -> p c d", p=P)),
            (wq[:, :, :], a["L1_xattn_wq"].rearrange("(c p) d -> p c d", p=P)),
            (wk[:, :, :], a["L1_xattn_wk"].rearrange("(c p) d -> p c d", p=P)),
            (wv[:, :, :], a["L1_xattn_wv"].rearrange("(c p) d -> p c d", p=P)),
            (wo[:, :, :], a["L1_xattn_wo"].rearrange("(c p) d -> p c d", p=P)),
            (gw[:, :, :], a["L1_ffn_gate_w"].rearrange("(c p) e -> p c e", p=P)),
            (b1_1[:, :], a["L1_ffn_b1"].rearrange("e h -> h e")),
            (b2_1[:, :], a["L1_ffn_b2"]),
            (w2_1[:, :, :], a["L1_ffn_w2"].rearrange("e h d -> h e d")),
        ]
        for c in range(C):
            loads.append((Wab[:, c, :], a["L0_attn_W_beta"][:, c * P:(c + 1) * P].rearrange("h p -> p h")))
            loads.append((rwT[:, c, :], a["L0_ffn_router_w"][:, c * P:(c + 1) * P].rearrange("e p -> p e")))
        for h in range(DH):
            loads.append((dw[:, 0, h, :], a["L0_attn_W_alpha"][h].partition_broadcast(P)))
            for n, name in enumerate(("L0_attn_A_log", "L0_attn_dt_bias")):
                loads.append((a_col[h:R:DH, n:n + 1], a[name][h:h + 1].partition_broadcast(NB)))
        for n, kind in enumerate(("q1", "q2", "k1", "k2", "v1", "v2")):
            loads.append((qw_raw[:, n * HD:(n + 1) * HD], a[f"L0_xattn_W{kind}"]))
            loads.append((qw_raw[:, 6 * HD + n:6 * HD + n + 1], a[f"L0_xattn_b{kind}"].unsqueeze(1)))
        for e in range(E0):
            loads.append((w1_0[:, e], a["L0_ffn_w1"][e].rearrange("(c p) h -> p c h", p=P)))
            loads.append((w2_0[:, e], a["L0_ffn_w2"][e].rearrange("(k p) d -> p k d", p=P)))
            loads.append((lng[:, e], a["L0_ffn_ln_g"][e].rearrange("(k p) -> p k", p=P)))
            loads.append((lnb[:, e], a["L0_ffn_ln_b"][e].rearrange("(k p) -> p k", p=P)))
        for e in range(E1):
            loads.append((w1_1[:, e], a["L1_ffn_w1"][e].rearrange("(c p) h -> p c h", p=P)))

        @block.sync
        def _(sp):
            for dst, src in loads:
                sp.dma_start(dst, src, allow_slow_non_contiguous=True).then_inc(w_loaded, 16)
            sp.dma_start(rx, x_r[0]).then_inc(loaded_r, 16)
            with sp.Fori(0, NPG * PG - 1) as n:
                sp.wait_ge(ref_x, n + 1)
                sp.dma_start(rx, x_r[n + 1]).then_inc(loaded_r, 16)
            sp.wait_ge(cum_ready, 1)
            sp.dma_start(cum_dram, cum_all[:, :]).then_inc(cum_stored, 16)
            sp.wait_ge(cum_stored, 16)

            def load_decays(it):
                sp.dma_start(crow[:, :, :, :].rearrange("p g h t -> p (g h t)"),
                             cum_dram.rearrange("(i r) t -> i (r t)", r=G * DH)[it].partition_broadcast(P)).then_inc(loaded_row, 16)

            load_decays(0)
            sp.dma_start(x_in[:, :, :], x_d[0]).then_inc(loaded_x, 16)
            sp.dma_start(ctx_in[:, :, :], ctx_d[0]).then_inc(loaded_c, 16)
            with sp.Fori(0, NIT - 1) as it:
                sp.wait_ge(S["ctx_psum"], at(it, "ctx_psum", 2))
                sp.dma_start(ctx_in[:, :, :], ctx_d[it + 1]).then_inc(loaded_c, 16)
                sp.wait_ge(S["dec_diff"], at(it, "dec_diff", 2))
                load_decays(it + 1)
                sp.wait_ge(S["xin_used"], at(it, "xin_used", 1))
                sp.dma_start(x_in[:, :, :], x_d[it + 1]).then_inc(loaded_x, 16)

        @block.gpsimd
        def _(pool):
            n_set = [0]

            def link(ins):
                n_set[0] += 1
                ins.then_inc(set_pool, 1)
                pool.wait_ge(set_pool, n_set[0])

            def select(t, pattern, base, mult, op, fill):
                link(pool.affine_select(out=t, in_=t, compare_op=op, fill=fill, base=base,
                                        pattern=pattern, channel_multiplier=mult))

            link(pool.memset(ones[:, :], 1.0))
            link(pool.memset(eps_ln[:, :], LN_EPS))
            link(pool.memset(ln_shift[:, :], 20.0 * 0.6931471805599453))
            link(pool.memset(ident[:, :], 0.0))
            select(ident[:, :], [[-1, P]], 0, 1, ALU.not_equal, 1.0)
            link(pool.tensor_copy(identb[:, :], ident[:, :]))
            link(pool.memset(strict[:, :], 1.0))
            select(strict[:, :], [[1, P]], -1, -1, ALU.is_ge, 0.0)
            for l in range(LEVELS + 1):
                n = 2 ** l
                t = same[:, l, :].rearrange("p (m n) -> p m n", n=n)
                link(pool.memset(same[:, l, :], 1.0))
                select(t, [[-n, P // n], [0, n]], 0, 1, ALU.is_ge, 0.0)
                select(t, [[n, P // n], [0, n]], n - 1, -1, ALU.is_ge, 0.0)
            for l in range(LEVELS):
                link(pool.tensor_tensor(levmask[:, l, :], same[:, l + 1, :], same[:, l, :], ALU.subtract))
            link(pool.memset(causal[:, :, :], 0.0))
            select(causal[:, :, :], [[0, QH], [-1, P]], 0, 1, ALU.is_ge, MASKED)
            link(pool.memset(headmask[:, :], 1.0))
            select(headmask[:, :], [[-HD, HPC]], 0, 1, ALU.is_ge, 0.0)
            select(headmask[:, :], [[HD, HPC]], HD - 1, -1, ALU.is_ge, 0.0)
            link(pool.memset(rep16[:, :, :], 0.0))
            select(rep16[:, :, :], [[0, HPC], [-1, HD]], 0, 1, ALU.not_equal, 1.0)
            link(pool.memset(rowsel[:, :, :], 0.0))
            select(rowsel[:, :, :], [[-1, DH], [0, P]], 0, 1, ALU.not_equal, 1.0)
            link(pool.memset(lo[:, :], 1.0))
            select(lo[:, :], [[0, 1]], CHUNK - 1, -1, ALU.is_ge, 0.0)
            link(pool.memset(resets[:, :], 1.0))
            link(pool.memset(resets[:, :].rearrange("p (m n) -> p m n", n=RUN)[:, :, 0:1], 0.0))
            link(pool.memset(run_resets[:, :], 1.0))
            link(pool.memset(run_resets[:, :].rearrange("p (m n) -> p m n", n=CHUNK // RUN)[:, :, 0:1], 0.0))
            link(pool.memset(run_sum[:, 0:1], 0.0))
            link(pool.memset(lt_mask[:, :, :], 1.0))
            select(lt_mask[:, :, :], [[1, E1], [-1, E1]], -1, 0, ALU.is_ge, 0.0)
            link(pool.memset(ge_mask[:, :, :], 1.0))
            select(ge_mask[:, :, :], [[-1, E1], [1, E1]], 0, 0, ALU.is_ge, 0.0)
            link(pool.memset(rkT[:, :, :, :], 0.0))
            pool.wait_ge(w_loaded, 16 * len(loads))
            link(pool.tensor_copy(Wkr[:, :, :], Wkv[:, 0:HD].unsqueeze(1).broadcast_to([P, HPC, HD])))
            assert n_set[0] == SET_POOL, n_set[0]
            pool.wait_ge(cum_ready, 1)
            pool.memset(V2[:, :, :, :], 1.0).then_inc(v_ones, 1)

            with pool.Fori(0, NIT) as it:
                pool.wait_ge(S["xn"], at(it, "xn", 4))
                pool.tensor_tensor(xres[:, :, :], x_in[:, :, :], xn[:, :, :], ALU.add).then_inc(S["xin_used"], 1)
                pool.wait_ge(S["dec_exp"], at(it, "dec_exp", 1))
                pool.tensor_tensor(dec[:, :, :].rearrange("p h (g t) -> p (h g) t", t=P),
                                   dec[:, :, :].rearrange("p h (g t) -> p (h g) t", t=P),
                                   strict[:, :].unsqueeze(1).broadcast_to([P, DH * G, P]), ALU.mult).then_inc(S["dec_strict"], 1)
                for l in range(LEVELS):
                    for h in range(DH):
                        if l == 0:
                            pool.wait_ge(S["MT"], at(it, "MT", h + 1))
                        if l == 2:
                            pool.wait_ge(S["inv_eye"], at(it, "inv_eye", h + 1))
                        if l > 2:
                            pool.wait_ge(S["W_psum"], at(it, "W_psum", 2 * (l - 3) + h + 1))
                        pool.tensor_tensor(heads(lev[:, l % 2, h, :]), heads(MT[:, h, :]),
                                           levmask[:, l, :].unsqueeze(1).broadcast_to([P, G, P]), ALU.mult).then_inc(S["lev"], 1)
                    if l == 0:
                        for h in range(DH):
                            pool.wait_ge(S["lev"], at(it, "lev", h + 1))
                            pool.tensor_tensor(heads(Um[:, h, :]), heads(lev[:, 0, h, :]), ident[:, :].unsqueeze(1).broadcast_to([P, G, P]), ALU.add).then_inc(S["inv_eye"], 1)
                pool.wait_ge(S["res"], at(it, "res", 2))
                pool.wait_ge(S["xn"], at(it, "xn", 8))
                pool.tensor_tensor(xres[:, :, :], xres[:, :, :], bo_row[:, :].unsqueeze(1).broadcast_to([P, G, D]), ALU.add).then_inc(S["bias_res"], 1)

                def mask_heads(att_no, first, chunks):
                    n = first
                    for g in range(G):
                        for c in range(chunks):
                            pool.wait_ge(S["k"], at(it, "k", K_BEFORE[att_no] + c + 1))
                            if g >= 2:
                                pool.wait_ge(S["s_psum"], at(it, "s_psum", att_no * QUADS + 4 * (g - 1)))
                            pool.tensor_tensor(KM[:, g % 2, c], KT[:, c, g * P:(g + 1) * P].unsqueeze(1).broadcast_to([P, HPC, P]),
                                               headmask[:, :].unsqueeze(2).broadcast_to([P, HPC, P]), ALU.mult).then_inc(S["km"], 1)
                            n += 1
                    return n
                n = mask_heads(0, 0, C)
                pool.wait_ge(S["xn"], at(it, "xn", 12))
                pool.tensor_tensor(xres[:, :, :], xres[:, :, :], onb_row[:, :].unsqueeze(1).broadcast_to([P, G, D]), ALU.add).then_inc(S["bias_res"], 1)
                pool.wait_ge(S["moe_g"], at(it, "moe_g", 4))
                pool.tensor_tensor(acc[:, :, :], acc[:, :, :], ong_row[:, :].unsqueeze(1).broadcast_to([P, G, D]), ALU.mult).then_inc(S["bias_res"], 1)
                n = mask_heads(1, n, 1)
                n = mask_heads(2, n, C)
                pool.wait_ge(stored, it * 16 + 16)

        @block.scalar
        def _(act):
            act.wait_ge(w_loaded, 16 * len(loads))
            act.wait_ge(set_pool, SET_POOL)
            act.preload_act_table_set(LN_EXP_TABLE)
            with act.Fori(0, NPG) as pg:
                for sub in range(PG):
                    n = pg * PG + sub
                    act.wait_ge(ref_var, n + 1)
                    act.activation(row[:, 2, :], row[:, 1, :], ACT.Ln).then_inc(ref_seed, 1)
                    act.wait_ge(ref_seed, n * 2 + 1)
                    act.activation(row[:, 3, :], row[:, 2, :], ACT.Exp, scale=0.5).then_inc(ref_seed, 1)

            with act.Fori(0, NIT) as it:
                def ln_rstd(n):
                    act.wait_ge(S["ln_var"], at(it, "ln_var", n + 1))
                    act.activation(lnv[:, :], mv[:, :, 1], ACT.Ln, scale=0.25, bias=eps_ln[:, 0:1]).then_inc(S["ln_log"], 1)
                    act.wait_ge(S["ln_log"], at(it, "ln_log", n + 1))
                    act.activation(rstd[:, :], lnv[:, :], ACT.Exp, scale=-0.5).then_inc(S["ln_rstd"], 1)

                def xT_copy(s):
                    act.wait_ge(S["xT_psum"], at(it, "xT_psum", 2 * s + 1))
                    act.activation(xT[:, 0, :], bank[0][:, :], ACT.Copy).then_inc(S["xT_act"], 1)

                act.preload_act_table_set(LN_EXP_TABLE)
                ln_rstd(0)
                xT_copy(0)
                for g in range(G):
                    for h in range(DH):
                        n = g * DH + h
                        act.activation(rk[:, n, :], xn[:, g, h * P:(h + 1) * P], ACT.Square, accum_out=ssq[:, n:n + 1]).then_inc(S["rk_sq"], 1)
                act.wait_ge(S["ab_psum"], at(it, "ab_psum", 1))
                act.activation(bet[:, :], bank[7][0:DH, :], ACT.Exp, scale=-1.0).then_inc(S["beta_exp"], 1)
                act.preload_act_table_set(LN_TABLE)
                act.wait_ge(S["rk_max"], at(it, "rk_max", 1))
                act.activation(rnl[:, :], ssq[:, :], ACT.Ln, scale=2.0 ** 40).then_inc(S["rk_log"], 1)
                act.preload_act_table_set(LN_EXP_TABLE)
                act.wait_ge(S["rk_log"], at(it, "rk_log", 1))
                act.activation(rns[:, :], rnl[:, :], ACT.Exp, scale=-0.5, bias=ln_shift[:, 0:1]).then_inc(S["rk_rs"], 1)
                act.wait_ge(S["ctx_psum"], at(it, "ctx_psum", 1))
                act.activation(ctxT[:, 0, :], bank[2][:, :], ACT.Copy).then_inc(S["ctxT_act"], 1)
                act.wait_ge(S["rk_psum"], at(it, "rk_psum", 1))
                act.activation(rkT[:, 0, :, 1:P + 1], heads(bank[4][:, :]), ACT.Copy).then_inc(S["rkT_act"], 1)
                act.wait_ge(S["dec_min"], at(it, "dec_min", 1))
                act.activation(dec[:, :, :], dec[:, :, :], ACT.Exp).then_inc(S["dec_exp"], 1)
                for l in range(LEVELS):
                    if l > 0:
                        for h in range(DH):
                            n = 2 * (l - 1) + h
                            act.wait_ge(S["W_psum"], at(it, "W_psum", n + 1))
                            act.activation(Wm[:, h, :], bank[2 + h][:, :], ACT.Copy).then_inc(S["W"], 1)
                    if l < LEVELS - 1:
                        for h in range(DH):
                            n = 2 * l + h
                            act.wait_ge(S["T_psum"], at(it, "T_psum", n + 1))
                            act.activation(Tm[:, h, :], bank[h][:, :], ACT.Copy).then_inc(S["T"], 1)
                for h in range(DH):
                    act.wait_ge(S["vnew_psum"], at(it, "vnew_psum", h + 1))
                    act.activation(vnew[:, h, :], bank[6 + h][:, :], ACT.Copy).then_inc(S["vnew"], 1)
                for h in range(DH):
                    act.wait_ge(S["oT_psum"], at(it, "oT_psum", h + 1))
                    act.activation(oT[:, h, :], bank[2 + h][:, :], ACT.Copy).then_inc(S["oT"], 1)

                def attention(a_no):
                    for u in range(QUADS + 8):
                        if u >= 2 and u - 2 < QUADS:
                            v = u - 2
                            act.wait_ge(S["s_sub"], at(it, "s_sub", a_no * QUADS + v + 1))
                            act.activation(Ssb[:, v % 4], Ssb[:, v % 4], ACT.Exp, scale=SCALE).then_inc(S["p_exp"], 1)
                        if u >= 3 and u - 3 < QUADS:
                            v = u - 3
                            act.wait_ge(S["t_psum"], at(it, "t_psum", a_no * QUADS + v + 1))
                            if v >= 2:
                                act.wait_ge(S["pv"], at(it, "pv", a_no * QUADS + v - 1))
                            act.activation(PT[:, v % 2], bank[3 + v % 2][:, :].rearrange("p (h q) -> p h q", h=QH), ACT.Copy).then_inc(S["pt"], 1)
                        if u >= 5 and (u - 5) % 4 == 3 and (u - 5) // 4 < G:
                            b = (u - 5) // 4
                            act.wait_ge(S["pv"], at(it, "pv", a_no * QUADS + 4 * b + 4))
                            act.activation(osb[:, b % 2, :], bank[5][:, :], ACT.Copy).then_inc(S["o_sb"], 1)
                        if u >= 7 and (u - 7) % 4 == 3 and (u - 7) // 4 < G:
                            b = (u - 7) // 4
                            act.wait_ge(S["attT_psum"], at(it, "attT_psum", a_no * G + b + 1))
                            act.activation(attT[:, :, b * P:(b + 1) * P],
                                           bank[6][:, 0:C * P].rearrange("p (c t) -> p c t", c=C), ACT.Copy).then_inc(S["attT"], 1)

                for n, k in enumerate((1, 2, 0)):
                    if k == 0:
                        act.preload_act_table_set(LN_EXP_TABLE)
                        ln_rstd(1)
                        xT_copy(1)
                    for c in range(C):
                        act.wait_ge(S["h_psum"], at(it, "h_psum", n * C + c + 1))
                        act.activation(hT[:, k, c, :], bank[(2, 4, 2)[k] + c][:, :], ACT.Tanh, bias=bcol[:, 2 * k:2 * k + 1]).then_inc(S["h_act"], 1)
                act.preload_act_table_set(LN_EXP_TABLE)
                attention(0)

                def gate_exp(n):
                    act.wait_ge(S["g_sub"], at(it, "g_sub", n + 1))
                    act.activation(gp[:, :, 0:(E0, E1)[n]], r_lg[:, :, 0:(E0, E1)[n]], ACT.Exp).then_inc(S["g_exp"], 1)

                ln_rstd(2)
                xT_copy(2)
                for e in range(E0 + 1):
                    if e < E0:
                        act.wait_ge(S["up_var"], at(it, "up_var", e + 1))
                        act.activation(ulg[:, :], umv[:, :, 1], ACT.Ln, scale=0.25, bias=eps_ln[:, 0:1]).then_inc(S["up_log"], 1)
                        act.wait_ge(S["up_log"], at(it, "up_log", e + 1))
                        act.activation(urs[:, :], ulg[:, :], ACT.Exp, scale=-0.5).then_inc(S["up_rstd"], 1)
                    if e > 0:
                        for k in range(KC0):
                            n = (e - 1) * KC0 + k
                            act.wait_ge(S["zT_psum"], at(it, "zT_psum", n + 1))
                            act.activation(zT[:, (e - 1) % 2, k, :], bank[4 + n % 2][:, :], ACT.Relu,
                                           scale=lng[:, e - 1, k:k + 1], bias=lnb[:, e - 1, k:k + 1]).then_inc(S["zT"], 1)
                    if e == 1:
                        ln_rstd(3)
                        gate_exp(0)
                ln_rstd(4)

                ln_rstd(5)
                xT_copy(3)
                act.wait_ge(S["lat_psum"], at(it, "lat_psum", 1))
                act.activation(latT[:, :], bank[2][:, :], ACT.Copy).then_inc(S["lat"], 1)
                attention(1)

                ln_rstd(6)
                xT_copy(4)
                attention(2)

                ln_rstd(7)
                xT_copy(5)
                gate_exp(1)
                for e in range(E1):
                    act.wait_ge(S["h1_psum"], at(it, "h1_psum", e + 1))
                    act.activation(h1[:, e, :], bank[2 + e % 2][:, :], ACT.Gelu, bias=b1_1[:, e:e + 1]).then_inc(S["h1"], 1)
                act.wait_ge(S["acc1"], at(it, "acc1", 34))
                act.dma_start(out_d[it], xres[:, :, :]).then_inc(stored, 16)
            act.wait_ge(stored, 16 * NIT)

        @block.tensor
        def _(pe):
            mm, tr = pe.matmul, pe.transpose
            pe.wait_ge(w_loaded, 16 * len(loads))
            pe.wait_ge(set_pool, SET_POOL)
            for m in range(2):
                for ce in range(C):
                    for cd in range(C):
                        ins = tr(bank[m][:, cd * D + ce * P:cd * D + ce * P + P], w_nat[:, m, ce, cd * P:(cd + 1) * P], ident[:, :])
            mm(bank[2][:, 0:6 * HD + 6], rep16[:, :, :].rearrange("p a b -> p (a b)"), qw_raw[:, :], start=True, stop=True).then_inc(set_pe, 1)
            pe.wait_ge(set_dve, 1)
            for c in range(C):
                ins = mm(bank[3][:, 0:2 * E0], ones[:, :], rgb[:, c].rearrange("p a e -> p (a e)"), start=(c == 0), stop=(c == C - 1))
            ins.then_inc(set_pe, 1)
            pe.wait_ge(set_dve, SET_DVE)
            pe.wait_ge(ref_step, REF_STEPS * NPG)
            tr(bank[0][0:R, 0:P], au[:, :], ident[:, :]).then_inc(au_psum, 1)
            pe.wait_ge(cum_ready, 1)
            tr(bank[1][:, 0:R], cum_all[:, :], ident[0:R, 0:R]).then_inc(cum_psum, 1)
            pe.wait_ge(v_ones, 1)
            pe.wait_ge(cum_ready, 2)

            with pe.Fori(0, NIT) as it:
                def to_features(s):
                    for c in range(C):
                        for g in range(G):
                            if c == 0:
                                pe.wait_ge(S["xn"], at(it, "xn", 4 * s + g + 1))
                            ins = tr(bank[c][:, g * P:(g + 1) * P], xn[:, g, c * P:(c + 1) * P], ident[:, :])
                        ins.then_inc(S["xT_psum"], 1)

                def xT_ready(s):
                    pe.wait_ge(S["xT_act"], at(it, "xT_act", s + 1))
                    pe.wait_ge(S["xT_dve"], at(it, "xT_dve", s + 1))

                to_features(0)
                pe.wait_ge(loaded_c, it * 16 + 16)
                for c in range(C):
                    for g in range(G):
                        ins = tr(bank[2 + c][:, g * P:(g + 1) * P], ctx_in[:, g, c * P:(c + 1) * P], ident[:, :])
                    ins.then_inc(S["ctx_psum"], 1)
                xT_ready(0)
                for c in range(C):
                    ins = mm(bank[7][0:DH, :], Wab[:, c, :], xT[:, c, :], start=(c == 0), stop=(c == C - 1))
                ins.then_inc(S["ab_psum"], 1)
                pe.wait_ge(S["rk"], at(it, "rk", 1))
                for h in range(DH):
                    for g in range(G):
                        ins = tr(bank[4 + h][:, g * P:(g + 1) * P], rk[:, g * DH + h, :], ident[:, :])
                    ins.then_inc(S["rk_psum"], 1)
                pe.wait_ge(S["rkT_act"], at(it, "rkT_act", 1))
                pe.wait_ge(S["rkT_dve"], at(it, "rkT_dve", 1))
                for h in range(DH):
                    for g in range(G):
                        ins = mm(bank[h][:, g * P:(g + 1) * P], rkT[:, h, g, 0:P], rkT[:, h, g, 0:P], start=True, stop=True)
                    ins.then_inc(S["G_psum"], 1)
                pe.wait_ge(S["beta"], at(it, "beta", 1))
                for h in range(DH):
                    mm(bank[4 + h][:, :], rowsel[:, h, :], bet[:, :], start=True, stop=True).then_inc(S["row_psum"], 1)
                pe.wait_ge(S["ctxT_dve"], at(it, "ctxT_dve", 1))
                mm(bank[6][:, 0:P], rowsel[:, 0, :], bet[:, 0:P], start=True, stop=True)
                for g in range(G):
                    ins = tr(bank[3][:, g * DH:(g + 1) * DH], bet[:, g * P:(g + 1) * P], ident[0:DH, 0:DH])
                ins.then_inc(S["col_psum"], 1)
                pe.wait_ge(S["ctxT_act"], at(it, "ctxT_act", 1))
                for h in range(DH):
                    if h == 1:
                        pe.wait_ge(S["col"], at(it, "col", 1))
                    for g in range(G):
                        ins = mm(bank[2 + h][:, g * P:(g + 1) * P], rkT[:, h, g, 0:P], rkT[:, h, g, 1:P + 1], start=True, stop=True)
                    ins.then_inc(S["R_psum"], 1)
                pe.wait_ge(S["dec_beta"], at(it, "dec_beta", 2))
                for g in range(G):
                    for c in range(C):
                        ins = mm(bank[4 + g // 2][:, (g % 2) * D:(g % 2 + 1) * D], xT[:, c, g * P:(g + 1) * P], WwT[:, c, :], start=(c == 0), stop=(c == C - 1))
                    if g % 2:
                        ins.then_inc(S["V_psum"], 1)
                for l in range(LEVELS):
                    if l > 0:
                        for h in range(DH):
                            n = 2 * (l - 1) + h
                            pe.wait_ge(S["lev"], at(it, "lev", 2 * l + h + 1))
                            pe.wait_ge(S["T"], at(it, "T", n + 1))
                            if l == 1:
                                pe.wait_ge(S["IT"], at(it, "IT", h + 1))
                            for g in range(G):
                                sl = slice(g * P, (g + 1) * P)
                                ins = mm(bank[2 + h][:, sl], lev[:, l % 2, h, sl], Tm[:, h, sl], start=True, stop=True)
                            ins.then_inc(S["W_psum"], 1)
                        for h in range(DH):
                            n = 2 * (l - 1) + h
                            pe.wait_ge(S["W"], at(it, "W", n + 1))
                            if l == 1:
                                pe.wait_ge(S["Vb"], at(it, "Vb", 2))
                            for g in range(G):
                                sl = slice(g * P, (g + 1) * P)
                                ins = mm(bank[4 + h][:, sl], Wm[:, h, sl], Um[:, h, sl], start=True, stop=True)
                            ins.then_inc(S["U_psum"], 1)
                    if l < LEVELS - 1:
                        for h in range(DH):
                            if l == 0:
                                pe.wait_ge(S["inv_eye"], at(it, "inv_eye", h + 1))
                            else:
                                pe.wait_ge(S["U"], at(it, "U", 2 * (l - 1) + h + 1))
                            for g in range(G):
                                sl = slice(g * P, (g + 1) * P)
                                ins = tr(bank[h][:, sl], Um[:, h, sl], ident[:, :])
                            ins.then_inc(S["T_psum"], 1)
                for h in range(DH):
                    pe.wait_ge(S["U"], at(it, "U", 2 * (LEVELS - 2) + h + 1))
                    for g in range(G):
                        sl = slice(g * P, (g + 1) * P)
                        ins = mm(bank[6 + h][:, sl], Um[:, h, sl], Vb[:, g, h * P:(h + 1) * P], start=True, stop=True)
                    ins.then_inc(S["vnew_psum"], 1)
                for h in range(DH):
                    pe.wait_ge(S["vnew"], at(it, "vnew", h + 1))
                    for g in range(G):
                        sl = slice(g * P, (g + 1) * P)
                        ins = mm(bank[2 + h][:, sl], vnew[:, h, sl], IT[:, h, sl], start=True, stop=True)
                    ins.then_inc(S["oT_psum"], 1)
                pe.wait_ge(S["oT"], at(it, "oT", 2))
                for g in range(G):
                    for h in range(DH):
                        ins = mm(bank[g // 2][:, (g % 2) * D:(g % 2 + 1) * D], oT[:, h, g * P:(g + 1) * P], WrT[:, h, :], start=(h == 0), stop=(h == DH - 1))
                    if g % 2:
                        ins.then_inc(S["y0_psum"], 1)

                def attention(a_no, masked, chunks, w_out):
                    base = a_no * QUADS
                    for u in range(QUADS + 8):
                        if u < QUADS:
                            g, c = u // 4, (u % 4) // 2
                            pe.wait_ge(S["km"], at(it, "km", KM_BEFORE[a_no] + g * chunks + min(c, chunks - 1) + 1))
                            if u >= 3:
                                pe.wait_ge(S["s_sub"], at(it, "s_sub", base + u - 2))
                            half = (u % 2) * QH
                            ins = mm(bank[u % 3][:, :], QT[:, c, g * P:(g + 1) * P],
                                     KM[:, g % 2, min(c, chunks - 1), half:half + QH, :].rearrange("p h t -> p (h t)"), start=True, stop=not masked)
                            if masked:
                                ins = mm(bank[u % 3][:, :], identb[:, :], causal[:, :, :].rearrange("p h t -> p (h t)"), start=False, stop=True)
                            ins.then_inc(S["s_psum"], 1)
                        if u >= 3 and u - 3 < QUADS:
                            v = u - 3
                            pe.wait_ge(S["p_exp"], at(it, "p_exp", base + v + 1))
                            if v >= 2:
                                pe.wait_ge(S["pt"], at(it, "pt", base + v - 1))
                            for j in range(QH):
                                ins = tr(bank[3 + v % 2][:, j * P:(j + 1) * P], Ssb[:, v % 4, j, :], ident[:, :])
                            ins.then_inc(S["t_psum"], 1)
                        if u >= 4 and u - 4 < QUADS:
                            v = u - 4
                            g = v // 4
                            pe.wait_ge(S["pt"], at(it, "pt", base + v + 1))
                            if v % 4 == 0 and g > 0:
                                pe.wait_ge(S["o_sb"], at(it, "o_sb", a_no * G + g))
                            for j in range(QH):
                                ins = mm(bank[5][2 * HD * j:2 * HD * (j + 1), (v % 4) * P:(v % 4 + 1) * P], V2[:, g, (v % 4) * QH + j, :], PT[:, v % 2, j, :], start=True, stop=True)
                            ins.then_inc(S["pv"], 1)
                        if u >= 6 and (u - 6) % 4 == 3 and (u - 6) // 4 < G:
                            b = (u - 6) // 4
                            pe.wait_ge(S["o_sb"], at(it, "o_sb", a_no * G + b + 1))
                            if b > 0:
                                pe.wait_ge(S["o_norm"], at(it, "o_norm", a_no * G + b))
                            for q in range(QH):
                                ins = tr(bank[7][:, q * P:(q + 1) * P], osb[:, b % 2, q * P:(q + 1) * P], ident[:, :])
                            ins.then_inc(S["otr_psum"], 1)
                        if u >= 7 and (u - 7) % 4 == 3 and (u - 7) // 4 < G:
                            att_features(a_no, (u - 7) // 4)
                    pe.wait_ge(S["attT"], at(it, "attT", a_no * G + G))
                    for g in range(G):
                        for c in range(C):
                            ins = mm(bank[g // 2][:, (g % 2) * D:(g % 2 + 1) * D], attT[:, c, g * P:(g + 1) * P], w_out[:, c, :], start=(c == 0), stop=(c == C - 1))
                        if g % 2:
                            ins.then_inc(S["y_psum"], 1)

                def att_features(a_no, b):
                    pe.wait_ge(S["o_norm"], at(it, "o_norm", a_no * G + b + 1))
                    if b > 0:
                        pe.wait_ge(S["attT"], at(it, "attT", a_no * G + b))
                    for c in range(C):
                        ins = tr(bank[6][:, c * P:(c + 1) * P], att[:, b % 2, c * HPC:(c + 1) * HPC, :].rearrange("p h d -> p (h d)"), ident[:, :])
                    ins.then_inc(S["attT_psum"], 1)

                def tanh_layer(k, banks, src):
                    for c in range(C):
                        mm(bank[banks + c][:, :], Wblk[:, 2 * k].rearrange("p a b -> p (a b)"), src[:, c, :], start=True, stop=True).then_inc(S["h_psum"], 1)

                tanh_layer(1, 4, ctxT)
                tanh_layer(2, 2, ctxT)
                for c in range(C):
                    pe.wait_ge(S["h_act"], at(it, "h_act", c + 1))
                    mm(bank[6 + c][:, :], Wblk[:, 3].rearrange("p a b -> p (a b)"), hT[:, 1, c, :], start=True, stop=True).then_inc(S["k_psum"], 1)
                pe.wait_ge(S["h_act"], at(it, "h_act", 4))
                for g in range(G):
                    for c in range(C):
                        ins = mm(bank[4 + g // 2][:, (g % 2) * D + c * P:(g % 2) * D + (c + 1) * P], hT[:, 2, c, g * P:(g + 1) * P], Wblk[:, 5].rearrange("p a b -> p (a b)"), start=True, stop=True)
                    if g % 2:
                        ins.then_inc(S["v_psum"], 1)
                pe.wait_ge(S["res"], at(it, "res", 2))
                to_features(1)
                xT_ready(1)
                tanh_layer(0, 2, xT)
                for c in range(C):
                    pe.wait_ge(S["h_act"], at(it, "h_act", 4 + c + 1))
                    mm(bank[2 + c][:, :], Wblk[:, 1].rearrange("p a b -> p (a b)"), hT[:, 0, c, :], start=True, stop=True).then_inc(S["q_psum"], 1)
                pe.wait_ge(S["q"], at(it, "q", 2))
                pe.wait_ge(S["v"], at(it, "v", 2))
                attention(0, False, C, Wo0)

                pe.wait_ge(S["res"], at(it, "res", 4))
                to_features(2)
                xT_ready(2)
                for g in range(G):
                    for c in range(C):
                        ins = mm(bank[7][:, g * E0:(g + 1) * E0], xT[:, c, g * P:(g + 1) * P], rgb[:, c, 0, :], start=(c == 0), stop=(c == C - 1))
                ins.then_inc(S["r_psum"], 1)
                for e in range(E0 + 1):
                    if e < E0:
                        for g in range(G):
                            if e > 0:
                                pe.wait_ge(S["z"], at(it, "z", 4 * (e - 1) + g + 1))
                            for c in range(C):
                                ins = mm(bank[g][:, :], xT[:, c, g * P:(g + 1) * P], w1_0[:, e, c, :], start=(c == 0), stop=(c == C - 1))
                            ins.then_inc(S["up_psum"], 1)
                    if e > 0:
                        for k in range(KC0):
                            n = (e - 1) * KC0 + k
                            if k == 0:
                                pe.wait_ge(S["z"], at(it, "z", 4 * e))
                            if n >= 2:
                                pe.wait_ge(S["zT"], at(it, "zT", n - 1))
                            for g in range(G):
                                ins = tr(bank[4 + n % 2][:, g * P:(g + 1) * P], z[:, (e - 1) % 2, g, k * P:(k + 1) * P], ident[:, :])
                            ins.then_inc(S["zT_psum"], 1)
                        pe.wait_ge(S["zT"], at(it, "zT", KC0 * e))
                        for g in range(G):
                            if g % 2 == 0:
                                if e > 1:
                                    pe.wait_ge(S["acc"], at(it, "acc", 4 * (e - 2) + g + 2))
                                else:
                                    pe.wait_ge(S["r_fix"], at(it, "r_fix", 1))
                            for k in range(KC0):
                                ins = mm(bank[6 + g // 2][:, (g % 2) * D:(g % 2 + 1) * D], zT[:, (e - 1) % 2, k, g * P:(g + 1) * P], w2_0[:, e - 1, k, :], start=(k == 0), stop=(k == KC0 - 1))
                            if g % 2:
                                ins.then_inc(S["dn_psum"], 1)

                to_features(3)
                xT_ready(3)
                for c in range(C):
                    ins = mm(bank[2][:, :], Wcd[:, c, :], xT[:, c, :], start=(c == 0), stop=(c == C - 1))
                ins.then_inc(S["lat_psum"], 1)
                pe.wait_ge(S["lat"], at(it, "lat", 1))
                mm(bank[3][:, :], Wkr[:, :, :].rearrange("p a b -> p (a b)"), latT[:, :], start=True, stop=True).then_inc(S["k_psum"], 1)
                for c in range(C):
                    mm(bank[4 + c][:, :], Wqu[:, c * P:(c + 1) * P], latT[:, :], start=True, stop=True).then_inc(S["q_psum"], 1)
                for g in range(G):
                    ins = mm(bank[2][:, g * HD:(g + 1) * HD], latT[:, g * P:(g + 1) * P], Wkv[:, HD:2 * HD], start=True, stop=True)
                ins.then_inc(S["v_psum"], 1)
                pe.wait_ge(S["q"], at(it, "q", 4))
                pe.wait_ge(S["v"], at(it, "v", 4))
                attention(1, True, 1, Wcp)

                for m in range(C):
                    for c in range(C):
                        ins = mm(bank[2 + m][:, :], wk[:, c, m * P:(m + 1) * P], ctxT[:, c, :], start=(c == 0), stop=(c == C - 1))
                    ins.then_inc(S["k_psum"], 1)
                for g in range(G):
                    for c in range(C):
                        ins = mm(bank[4 + g // 2][:, (g % 2) * D:(g % 2 + 1) * D], ctxT[:, c, g * P:(g + 1) * P], wv[:, c, :], start=(c == 0), stop=(c == C - 1))
                    if g % 2:
                        ins.then_inc(S["v_psum"], 1)
                to_features(4)
                xT_ready(4)
                for m in range(C):
                    for c in range(C):
                        ins = mm(bank[6 + m][:, :], wq[:, c, m * P:(m + 1) * P], xT[:, c, :], start=(c == 0), stop=(c == C - 1))
                    ins.then_inc(S["q_psum"], 1)
                pe.wait_ge(S["q"], at(it, "q", 6))
                pe.wait_ge(S["v"], at(it, "v", 6))
                attention(2, True, C, wo)

                to_features(5)
                xT_ready(5)
                for g in range(G):
                    for c in range(C):
                        ins = mm(bank[6][:, g * E1:(g + 1) * E1], xT[:, c, g * P:(g + 1) * P], gw[:, c, :], start=(c == 0), stop=(c == C - 1))
                ins.then_inc(S["gl_psum"], 1)
                for e in range(E1):
                    if e >= 2:
                        pe.wait_ge(S["h1"], at(it, "h1", e - 1))
                    for c in range(C):
                        ins = mm(bank[2 + e % 2][:, :], w1_1[:, e, c, :], xT[:, c, :], start=(c == 0), stop=(c == C - 1))
                    ins.then_inc(S["h1_psum"], 1)
                pe.wait_ge(S["g_w"], at(it, "g_w", 2))
                for g in range(G):
                    ins = tr(bank[7][0:E1, g * P:(g + 1) * P], gate[:, g, :], ident[:, :])
                ins.then_inc(S["gT_psum"], 1)
                pe.wait_ge(S["gT"], at(it, "gT", 1))
                for g in range(G):
                    ins = mm(bank[g // 2][:, (g % 2) * D:(g % 2 + 1) * D], gT[:, g * P:(g + 1) * P], b2_1[:, :], start=True, stop=True)
                    if g % 2:
                        ins.then_inc(S["b2_psum"], 1)
                for e in range(E1):
                    pe.wait_ge(S["h1"], at(it, "h1", e + 1))
                    for g in range(G):
                        n = 2 * e + g // 2
                        if g % 2 == 0 and n >= 4:
                            pe.wait_ge(S["acc1"], at(it, "acc1", 2 + 2 * (n - 4) + 2))
                        ins = mm(bank[4 + n % 4][:, (g % 2) * D:(g % 2 + 1) * D], h1[:, e, g * P:(g + 1) * P], w2_1[:, e, :], start=True, stop=True)
                        if g % 2:
                            ins.then_inc(S["y1_psum"], 1)
                pe.wait_ge(S["acc1"], at(it, "acc1", 34))

        def decay_phase(dve):
            tt, ts, stt = dve.tensor_tensor, dve.tensor_scalar, dve.scalar_tensor_tensor
            MUL, ADD, SUB = ALU.mult, ALU.add, ALU.subtract

            with dve.Fori(0, NPG) as pg:
                n_ref = [0]

                def step(ins):
                    n_ref[0] += 1
                    ins.then_inc(ref_step, 1)
                    dve.wait_ge(ref_step, pg * REF_STEPS + n_ref[0])

                def by_row(do):
                    for b in range(PB):
                        ins = do(b)
                        if b < PB - 1:
                            n_ref[0] += 1
                            ins.then_inc(ref_step, 1)
                    step(ins)

                def halves(src, t, high, low):
                    step(ts(t, src, SPLIT, None, MUL))
                    step(tt(high, t, src, SUB))
                    step(tt(high, t, high, SUB))
                    step(tt(low, src, high, SUB))

                r = lambda n: row[:, n, :]
                for sub in range(PG):
                    dve.wait_ge(loaded_r, (pg * PG + sub) * 16 + 16)
                    step(tt(lan[:, :, :], rx[:, :, 0:16], rx[:, :, 16:32], ADD))
                    for k in range(2, D // 16):
                        step(tt(lan[:, :, :], lan[:, :, :], rx[:, :, 16 * k:16 * k + 16], ADD))
                    l4 = lan[:, :, :].rearrange("p b (c d) -> p b c d", d=4)
                    m4 = lan2[:, :, :].rearrange("p b (c d) -> p b c d", d=4)
                    step(tt(m4, l4[:, :, 0:4:2, :], l4[:, :, 1:4:2, :], ADD))
                    step(tt(lan[:, :, 0:4], lan2[:, :, 0:4], lan2[:, :, 4:8], ADD))
                    step(tt(lan2[:, :, 0:2], lan[:, :, 0:4:2], lan[:, :, 1:4:2], ADD))
                    step(tt(r(0), lan2[:, :, 0], lan2[:, :, 1], ADD))
                    step(ts(r(0), r(0), 1.0 / D, None, MUL))
                    step(tt(rx, rx, r(0).unsqueeze(2).broadcast_to([P, PB, D]), SUB))
                    step(tt(rt, rx, rx, MUL))
                    w8 = rt.rearrange("p b (k n) -> p b k n", n=32)
                    step(tt(lan2[:, :, :], w8[:, :, :, 0], w8[:, :, :, 1], ADD))
                    for k in range(2, 32):
                        step(tt(lan2[:, :, :], lan2[:, :, :], w8[:, :, :, k], ADD))
                    step(tt(lan[:, :, 0:4], lan2[:, :, 0:4], lan2[:, :, 4:8], ADD))
                    step(tt(lan2[:, :, 0:2], lan[:, :, 0:4:2], lan[:, :, 1:4:2], ADD))
                    step(tt(r(1), lan2[:, :, 0], lan2[:, :, 1], ADD))
                    ts(r(1), r(1), 1.0 / D, LN_EPS, MUL, ADD).then_inc(ref_var, 1)
                    dve.wait_ge(ref_seed, (pg * PG + sub) * 2 + 2)
                    step(dve.reciprocal(r(4), r(3)))
                    step(tt(r(4), r(1), r(4), MUL))
                    step(tt(r(4), r(4), r(3), ADD))
                    step(ts(r(4), r(4), 0.5, None, MUL))
                    step(dve.reciprocal(r(5), r(4)))
                    halves(r(4), r(6), r(7), r(8))
                    step(tt(r(9), r(4), r(4), MUL))
                    step(tt(r(10), r(7), r(7), MUL))
                    step(tt(r(10), r(10), r(9), SUB))
                    step(tt(r(11), r(7), r(8), MUL))
                    step(tt(r(10), r(10), r(11), ADD))
                    step(tt(r(10), r(10), r(11), ADD))
                    step(tt(r(11), r(8), r(8), MUL))
                    step(tt(r(10), r(10), r(11), ADD))
                    step(tt(r(9), r(1), r(9), SUB))
                    step(tt(r(9), r(9), r(10), SUB))
                    step(stt(out=r(9), in0=r(9), scalar=0.5, in1=r(5), op0=MUL, op1=MUL))
                    step(tt(r(4), r(4), r(9), ADD))
                    step(dve.reciprocal(r(5), r(4)))
                    halves(r(4), r(6), r(7), r(8))
                    q, p_, e_ = rp[:, sub, 0], rp[:, sub, 1], re[:, sub, 0]
                    one = lambda n, b: row[:, n, b:b + 1]
                    by_row(lambda b: ts(q[:, b, :], rx[:, b, :], one(5, b), None, MUL))
                    halves(q, rt, rh, rl)
                    by_row(lambda b: ts(p_[:, b, :], q[:, b, :], one(4, b), None, MUL))
                    by_row(lambda b: stt(out=e_[:, b, :], in0=rh[:, b, :], scalar=one(7, b), in1=p_[:, b, :], op0=MUL, op1=SUB))
                    by_row(lambda b: stt(out=e_[:, b, :], in0=rh[:, b, :], scalar=one(8, b), in1=e_[:, b, :], op0=MUL, op1=ADD))
                    by_row(lambda b: stt(out=e_[:, b, :], in0=rl[:, b, :], scalar=one(7, b), in1=e_[:, b, :], op0=MUL, op1=ADD))
                    by_row(lambda b: stt(out=e_[:, b, :], in0=rl[:, b, :], scalar=one(8, b), in1=e_[:, b, :], op0=MUL, op1=ADD))
                    step(tt(rx, rx, p_, SUB))
                    step(tt(rx, rx, e_, SUB))
                    by_row(lambda b: stt(out=rx[:, b, :], in0=rx[:, b, :], scalar=one(5, b), in1=q[:, b, :], op0=MUL, op1=ADD))
                    halves(rx, rt, rh, rl)
                    for h in range(DH):
                        w, wh, wl = (dw[:, k, h, :].unsqueeze(1).broadcast_to([P, PB, D]) for k in range(3))
                        p_, e_ = rp[:, sub, h], re[:, sub, h]
                        last = tt(p_, rx, w, MUL)
                        step(last)
                        step(tt(e_, rh, wh, MUL))
                        step(tt(e_, e_, p_, SUB))
                        for a1, b1 in ((rh, wl), (rl, wh), (rl, wl)):
                            step(tt(rt, a1, b1, MUL))
                            ins = tt(e_, e_, rt, ADD)
                            if h == DH - 1 and a1 is rl and b1 is wl:
                                ins.then_inc(ref_x, 1)
                                dve.wait_ge(ref_x, pg * PG + sub + 1)
                            else:
                                step(ins)
                pf = rp.rearrange("p s h b d -> p (s h b) d")
                ef = re.rearrange("p s h b d -> p (s h b) d")
                n_ref[0] += 1
                dve.tensor_copy(acc_s, pf[:, :, 0:LANES]).then_inc(ref_step, 1)
                before = n_ref[0]
                per = 8
                with dve.Fori(0, (D // LANES - 1) // UNROLL) as j:
                    count = [0]

                    def link(operation, *operands):
                        dve.wait_ge(ref_step, pg * REF_STEPS + j * (UNROLL * per) + (before + count[0]))
                        operation(*operands).then_inc(ref_step, 1)
                        count[0] += 1

                    for k in range(UNROLL):
                        at_ = bass.ds(j * (UNROLL * LANES) + (k + 1) * LANES, LANES)
                        pj, ej = pf[:, :, at_], ef[:, :, at_]
                        link(tt, acc_a, acc_s, pj, ADD)
                        link(tt, acc_b, acc_a, acc_s, SUB)
                        link(tt, acc_c, acc_a, acc_b, SUB)
                        link(tt, acc_d, pj, acc_b, SUB)
                        link(tt, acc_c, acc_s, acc_c, SUB)
                        link(tt, acc_c, acc_c, acc_d, ADD)
                        link(tt, acc_c, acc_c, ej, ADD)
                        link(tt, acc_s, acc_a, acc_c, ADD)
                n_ref[0] += (D // LANES - 1) * per
                dve.wait_ge(ref_step, pg * REF_STEPS + n_ref[0])
                step(tt(acc_a[:, :, 0:2], acc_s[:, :, 0:4:2], acc_s[:, :, 1:4:2], ADD))
                n_ref[0] += 1
                tt(au[:, bass.ds(pg * (PG * PB * DH), PG * PB * DH)].rearrange("p (s b h) -> p s h b", s=PG, h=DH),
                        acc_a[:, :, 0].rearrange("p (s h b) -> p s h b", s=PG, h=DH), acc_a[:, :, 1].rearrange("p (s h b) -> p s h b", s=PG, h=DH), ADD).then_inc(ref_step, 1)
                assert n_ref[0] == REF_STEPS, n_ref[0]

            n_dec = [0]

            def step(ins):
                n_dec[0] += 1
                ins.then_inc(decay_step, 1)
                dve.wait_ge(decay_step, n_dec[0])

            u, t, n_, a_, b_, r_, lo_, r2, q_, h_ = dec_t[0:10]
            dve.wait_ge(au_psum, 1)
            step(ts(u[:, 0:P], bank[0][0:R, 0:P], a_col[:, 1:2], None, ADD))
            step(stt(out=t[:, 0:P], in0=u[:, 0:P], scalar=-1.0, in1=u[:, 0:P], op0=MUL, op1=ALU.min))
            step(ts(t[:, 0:P], t[:, 0:P], -86.0, None, ALU.max))
            step(dve.tensor_copy(t[:, P:P + 1], a_col[:, 0:1]))
            step(ts(n_, t, 1.4426950408889634, 12582912.0, MUL, ADD))
            step(ts(n_, n_, -12582912.0, None, ADD))
            step(stt(out=a_, in0=n_, scalar=-0.693359375, in1=t, op0=MUL, op1=ADD))
            step(ts(b_, n_, -2.12194440e-4, None, MUL))
            step(tt(r_, a_, b_, SUB))
            step(tt(lo_, a_, r_, SUB))
            step(tt(lo_, lo_, b_, SUB))
            step(tt(r2, r_, r_, MUL))
            step(ts(q_, r_, 1 / 5040, 1 / 720, MUL, ADD))
            for c in (1 / 120, 1 / 24, 1 / 6, 1 / 2):
                step(tt(q_, q_, r_, MUL))
                step(ts(q_, q_, c, None, ADD))
            step(tt(q_, q_, r2, MUL))
            step(tt(q_, q_, lo_, ADD))
            step(ts(h_, r_, 1.0, None, ADD))
            step(ts(a_, h_, -1.0, None, ADD))
            step(tt(a_, r_, a_, SUB))
            step(tt(q_, a_, q_, ADD))
            eh, el = dec_t[10:12]
            step(tt(eh, h_, q_, ADD))
            step(tt(el, eh, h_, SUB))
            step(tt(el, q_, el, SUB))
            two_n = dec_t[12].bitcast(mybir.dt.int32)
            step(ts(two_n, n_, 127.0, None, ADD))
            step(dve.tensor_scalar(two_n, two_n, 23, None, ALU.logical_shift_left))
            step(tt(eh, eh, dec_t[12], MUL))
            step(tt(el, el, dec_t[12], MUL))
            E, El, dh_, dl_, rec, s_, p_, x_, y_, z_ = (k[:, 0:P] for k in (eh, el, *dec_t[2:10]))
            sh, sl, vh, vl, sc = (k[:, 0:P] for k in dec_t[12:17])
            step(ts(dh_, E, 2.0, None, ADD))
            step(ts(x_, dh_, -2.0, None, ADD))
            step(tt(x_, E, x_, SUB))
            step(tt(dl_, x_, El, ADD))
            step(dve.reciprocal(rec, dh_))
            step(tt(s_, E, rec, MUL))
            for src, high, low in ((s_, sh, sl), (dh_, vh, vl)):
                step(ts(x_, src, SPLIT, None, MUL))
                step(tt(high, x_, src, SUB))
                step(tt(high, x_, high, SUB))
                step(tt(low, src, high, SUB))
            step(tt(p_, s_, dh_, MUL))
            step(tt(y_, sh, vh, MUL))
            step(tt(y_, y_, p_, SUB))
            for a1, b1 in ((sh, vl), (sl, vh), (sl, vl)):
                step(tt(x_, a1, b1, MUL))
                step(tt(y_, y_, x_, ADD))
            step(tt(x_, E, p_, SUB))
            step(tt(x_, x_, y_, SUB))
            step(tt(x_, x_, El, ADD))
            step(tt(y_, s_, dl_, MUL))
            step(tt(x_, x_, y_, SUB))
            step(tt(x_, x_, rec, MUL))
            step(tt(z_, s_, s_, MUL))
            step(ts(y_, z_, 1 / 17, 1 / 15, MUL, ADD))
            for c in (1 / 13, 1 / 11, 1 / 9, 1 / 7, 1 / 5, 1 / 3):
                step(tt(y_, y_, z_, MUL))
                step(ts(y_, y_, c, None, ADD))
            step(tt(z_, z_, s_, MUL))
            step(tt(y_, y_, z_, MUL))
            step(tt(y_, y_, x_, ADD))
            step(tt(y_, y_, s_, ADD))
            step(ts(y_, y_, 2.0, None, MUL))
            step(stt(out=y_, in0=u[:, 0:P], scalar=0.0, in1=y_, op0=ALU.max, op1=ADD))
            step(ts(y_, y_, eh[:, P:P + 1], -1.0, MUL, MUL))
            step(dve.tensor_tensor_scan(cum_all[:, :], resets[:, :], y_, 0.0, MUL, ADD))
            runs = cum_all[:, :].rearrange("p (m n) -> p m n", n=RUN)
            step(dve.tensor_tensor_scan(run_sum[:, 1:], run_resets[:, :], runs[:, :, RUN - 1], 0.0, MUL, ADD))
            step(tt(run_pre[:, :], run_sum[:, 0:P // RUN], run_resets[:, :], MUL))
            tt(runs, runs, run_pre[:, :].unsqueeze(2).broadcast_to([R, P // RUN, RUN]), ADD).then_inc(cum_ready, 1)
            dve.wait_ge(cum_psum, 1)
            dve.tensor_copy(colcum[:, :], bank[1][:, 0:R]).then_inc(cum_ready, 1)
            dve.wait_ge(cum_ready, 2)

        @block.vector
        def _(dve):
            n_set = [0]

            def link(ins):
                n_set[0] += 1
                ins.then_inc(set_dve, 1)
                dve.wait_ge(set_dve, n_set[0])

            dve.wait_ge(w_loaded, 16 * len(loads))
            dve.wait_ge(set_pool, SET_POOL)
            dve.tensor_tensor(rgb[:, :, 0, :], rwT[:, :, :], rn_g[:, :].unsqueeze(2).broadcast_to([P, C, E0]), ALU.mult)
            link(dve.tensor_tensor(rgb[:, :, 1, :], rwT[:, :, :], rn_b[:, :].unsqueeze(2).broadcast_to([P, C, E0]), ALU.mult))
            for src, dst, other in ((dw[:, 0], dw[:, 1], dw[:, 2]),):
                link(dve.tensor_scalar(other, src, SPLIT, None, ALU.mult))
                link(dve.tensor_tensor(dst, other, src, ALU.subtract))
                link(dve.tensor_tensor(dst, other, dst, ALU.subtract))
                link(dve.tensor_tensor(other, src, dst, ALU.subtract))
            dve.wait_ge(set_pe, 1)
            link(dve.tensor_copy(WwT[:, :, :].rearrange("p c d -> p (c d)"), bank[0][:, :]))
            link(dve.tensor_copy(WrT[:, :, :].rearrange("p c d -> p (c d)"), bank[1][:, :]))
            for n in range(6):
                link(dve.tensor_tensor(Wblk[:, n], bank[2][:, n * HD:(n + 1) * HD].unsqueeze(1).broadcast_to([P, HPC, HD]),
                                       headmask[:, :].unsqueeze(2).broadcast_to([P, HPC, HD]), ALU.mult))
            link(dve.tensor_copy(bcol[:, :], bank[2][:, 6 * HD:6 * HD + 6]))
            dve.wait_ge(set_pe, 2)
            link(dve.tensor_copy(rsum[:, :, :].rearrange("p a e -> p (a e)"), bank[3][:, 0:2 * E0]))
            assert n_set[0] == SET_DVE, n_set[0]
            decay_phase(dve)

            with dve.Fori(0, NIT) as it:
                def wait(name, n):
                    dve.wait_ge(S[name], at(it, name, n))

                def row_moments(st, pt, out, n, name, width):
                    dve.tensor_tensor(pt[:, 0, :], st[:, :, 1], st[:, :, 4], ALU.add).then_inc(S[name + "_parts"], 1)
                    dve.tensor_tensor(pt[:, 1, :], st[:, :, 1], st[:, :, 4], ALU.subtract).then_inc(S[name + "_parts"], 1)
                    dve.tensor_tensor(pt[:, 2, :], st[:, :, 2], st[:, :, 5], ALU.add).then_inc(S[name + "_parts"], 1)
                    wait(name + "_parts", 3 * n + 3)
                    dve.tensor_scalar(out[:, :, 0], pt[:, 0, :], 0.5, None, ALU.mult).then_inc(S[name + "_mean"], 1)
                    dve.tensor_tensor(pt[:, 3, :], pt[:, 1, :], pt[:, 1, :], ALU.mult).then_inc(S[name + "_mean"], 1)
                    wait(name + "_mean", 2 * n + 2)
                    dve.scalar_tensor_tensor(out=out[:, :, 1], in0=pt[:, 2, :], scalar=4.0 / width, in1=pt[:, 3, :], op0=ALU.mult, op1=ALU.add).then_inc(S[name + "_var"], 1)

                def refine(rs, out, pt, n, name):
                    fix = lambda ins, k: (ins.then_inc(S[name + "_fix"], 1), wait(name + "_fix", 5 * n + k))
                    wait(name + "_var", n + 1)
                    fix(dve.tensor_scalar(pt[:, 2, :], out[:, :, 1], 0.25, LN_EPS, ALU.mult, ALU.add), 1)
                    wait(name + "_rstd", n + 1)
                    fix(dve.tensor_tensor(pt[:, 0, :], rs[:, :], rs[:, :], ALU.mult), 2)
                    fix(dve.tensor_tensor(pt[:, 0, :], pt[:, 0, :], pt[:, 2, :], ALU.mult), 3)
                    fix(dve.tensor_scalar(pt[:, 0, :], pt[:, 0, :], -0.5, 1.5, ALU.mult, ALU.add), 4)
                    fix(dve.tensor_tensor(rs[:, :], rs[:, :], pt[:, 0, :], ALU.mult), 5)

                def row_stats(n, src, ready):
                    for g in range(G):
                        if ready:
                            ready(g)
                        dve.bn_stats(stats[:, g, :], src[:, g, :]).then_inc(S["ln_stats"], 1)
                    wait("ln_stats", 4 * n + 4)
                    row_moments(stats, parts, mv, n, "ln", D)

                def normalise(n, dst, src, signal):
                    refine(rstd, mv, parts, n, "ln")
                    for g in range(G):
                        dve.tensor_scalar(dst[:, g, :], src[:, g, :], mv[:, g, 0:1], rstd[:, g:g + 1], ALU.subtract, ALU.mult).then_inc(S[signal], 1)

                def layer_norm(s, n, src, ready):
                    row_stats(n, src, ready)
                    normalise(n, xn, src, "xn")

                def xT_copy(s):
                    wait("xT_psum", 2 * s + 2)
                    dve.tensor_copy(xT[:, 1, :], bank[1][:, :]).then_inc(S["xT_dve"], 1)

                dve.wait_ge(loaded_x, it * 16 + 16)
                layer_norm(0, 0, x_in, None)
                xT_copy(0)
                wait("rk_sq", 8)
                dve.tensor_scalar(ssq[:, :], ssq[:, :], 1e-24, None, ALU.max).then_inc(S["rk_max"], 1)
                wait("rk_rs", 1)
                dve.tensor_tensor(rk[:, :, :], xn[:, :, :].rearrange("p g (h t) -> p (g h) t", h=DH),
                                  rns[:, :].unsqueeze(2).broadcast_to([P, G * DH, P]), ALU.mult).then_inc(S["rk"], 1)
                wait("ctx_psum", 2)
                dve.tensor_copy(ctxT[:, 1, :], bank[3][:, :]).then_inc(S["ctxT_dve"], 1)
                wait("beta_exp", 1)
                dve.tensor_scalar(bet[:, :], bet[:, :], 1.0, None, ALU.add).then_inc(S["beta_1p"], 1)
                wait("beta_1p", 1)
                dve.reciprocal(bet[:, :], bet[:, :]).then_inc(S["beta"], 1)
                wait("rk_psum", 2)
                dve.tensor_copy(rkT[:, 1, :, 1:P + 1], heads(bank[5][:, :])).then_inc(S["rkT_dve"], 1)
                wait("col_psum", 1)
                dve.tensor_copy(col[:, :, :].rearrange("p g h -> p (g h)"), bank[3][:, 0:G * DH]).then_inc(S["col"], 1)
                mine = colcum[:, bass.ds(it * (G * DH), G * DH)].rearrange("p (g h) -> p h g", h=DH)
                dve.tensor_scalar(off[:, :, :, :], mine.unsqueeze(3).broadcast_to([P, DH, G, 2]), -1.0, None, ALU.mult).then_inc(S["dec_neg"], 1)
                dve.wait_ge(loaded_row, it * 16 + 16)
                wait("dec_neg", 1)
                for h in range(DH):
                    dve.scalar_tensor_tensor(out=off[:, h, :, 1], in0=crow[:, :, h, CHUNK - 1], scalar=lo[:, 0:1], in1=off[:, h, :, 1], op0=ALU.mult, op1=ALU.add).then_inc(S["dec_off"], 1)
                for h in range(DH):
                    wait("dec_off", h + 1)
                    dve.tensor_tensor(dec[:, h, :].rearrange("p (g k n) -> p g k n", k=2, n=CHUNK), crow[:, :, h, :].rearrange("p g (k n) -> p g k n", n=CHUNK),
                                      off[:, h, :, :].unsqueeze(3).broadcast_to([P, G, 2, CHUNK]), ALU.add).then_inc(S["dec_diff"], 1)
                wait("dec_diff", 2)
                dve.tensor_scalar(dec[:, :, :], dec[:, :, :], 0.0, None, ALU.min).then_inc(S["dec_min"], 1)
                wait("dec_strict", 1)
                for h in range(DH):
                    wait("row_psum", h + 1)
                    dve.scalar_tensor_tensor(out=decb[:, h, :], in0=bank[4 + h][:, :], scalar=-1.0, in1=dec[:, h, :], op0=ALU.mult, op1=ALU.mult).then_inc(S["dec_beta"], 1)
                for h in range(DH):
                    wait("G_psum", h + 1)
                    wait("dec_beta", h + 1)
                    dve.tensor_tensor(MT[:, h, :], bank[h][:, :], decb[:, h, :], ALU.mult).then_inc(S["MT"], 1)
                for h in range(DH):
                    wait("R_psum", h + 1)
                    dve.tensor_tensor(IT[:, h, :], bank[2 + h][:, :], dec[:, h, :], ALU.mult).then_inc(S["IT"], 1)
                for m in range(2):
                    wait("V_psum", m + 1)
                    for g in (2 * m, 2 * m + 1):
                        ins = dve.tensor_tensor(Vb[:, g, :].rearrange("p (h t) -> p h t", h=DH), bank[4 + m][:, (g % 2) * D:(g % 2 + 1) * D].rearrange("p (h t) -> p h t", h=DH),
                                                col[:, g, :].unsqueeze(2).broadcast_to([P, DH, P]), ALU.mult)
                    ins.then_inc(S["Vb"], 1)
                for l in range(1, LEVELS):
                    for h in range(DH):
                        wait("U_psum", 2 * (l - 1) + h + 1)
                        dve.tensor_tensor(Um[:, h, :], Um[:, h, :], bank[4 + h][:, :], ALU.add).then_inc(S["U"], 1)
                wait("xin_used", 1)
                for m in range(2):
                    wait("y0_psum", m + 1)
                    dve.tensor_tensor(xres[:, 2 * m:2 * m + 2, :].rearrange("p g d -> p (g d)"), xres[:, 2 * m:2 * m + 2, :].rearrange("p g d -> p (g d)"), bank[m][:, :], ALU.add).then_inc(S["res"], 1)

                def attention(a_no):
                    base = a_no * QUADS
                    for u in range(QUADS + 8):
                        if u < QUADS:
                            wait("s_psum", base + u + 1)
                            sc = bank[u % 3][:, :].rearrange("p (h k) -> p h k", h=QH)
                            dve.tensor_reduce(smax[:, u, :], sc, AX, ALU.max).then_inc(S["s_max"], 1)
                            wait("s_max", base + u + 1)
                            if u >= 4:
                                wait("t_psum", base + u - 3)
                            dve.tensor_tensor(Ssb[:, u % 4], sc, smax[:, u, :].unsqueeze(2).broadcast_to([P, QH, P]), ALU.subtract).then_inc(S["s_sub"], 1)
                        if u >= 6 and (u - 6) % 4 == 3 and (u - 6) // 4 < G:
                            b = (u - 6) // 4
                            wait("otr_psum", a_no * G + b + 1)
                            o = bank[7][:, :].rearrange("p (h d) -> p h d", d=2 * HD)
                            dve.reciprocal(orec[:, b, :], o[:, :, HD]).then_inc(S["o_rec"], 1)
                            wait("o_rec", a_no * G + b + 1)
                            dve.tensor_tensor(att[:, b % 2], o[:, :, 0:HD], orec[:, b, :].unsqueeze(2).broadcast_to([P, NH, HD]), ALU.mult).then_inc(S["o_norm"], 1)

                def add_y(a_no, first):
                    for m in range(2):
                        wait("y_psum", 2 * a_no + m + 1)
                        dve.tensor_tensor(xres[:, 2 * m:2 * m + 2, :].rearrange("p g d -> p (g d)"), xres[:, 2 * m:2 * m + 2, :].rearrange("p g d -> p (g d)"), bank[m][:, :], ALU.add).then_inc(S["res"], 1)

                def v_heads(m, bias):
                    dst = V2[:, 2 * m:2 * m + 2, :, 0:HD].rearrange("p g h d -> p (g h) d")
                    src = bank[4 + m][:, :].rearrange("p (n d) -> p n d", d=HD)
                    if bias:
                        return dve.tensor_tensor(dst, src, bv2_row[:, :].unsqueeze(1).broadcast_to([P, 2 * NH, HD]), ALU.add)
                    return dve.tensor_copy(dst, src)

                layer_norm(1, 1, xres, lambda g: wait("res", g // 2 + 1))
                xT_copy(1)
                for c in range(C):
                    wait("k_psum", c + 1)
                    dve.tensor_scalar(KT[:, c, :], bank[6 + c][:, :], bcol[:, 3:4], None, ALU.add).then_inc(S["k"], 1)
                for m in range(2):
                    wait("v_psum", m + 1)
                    v_heads(m, True).then_inc(S["v"], 1)
                for c in range(C):
                    wait("q_psum", c + 1)
                    dve.tensor_scalar(QT[:, c, :], bank[2 + c][:, :], bcol[:, 1:2], None, ALU.add).then_inc(S["q"], 1)
                attention(0)
                wait("bias_res", 1)
                add_y(0, 2)

                def gates(n, E):
                    wait_rank = lambda name: wait(name, n + 1)
                    dve.tensor_reduce(gmx[:, :], r_raw[:, :, 0:E], AX, ALU.max).then_inc(S["g_max"], 1)
                    wait_rank("g_max")
                    dve.tensor_tensor(r_lg[:, :, 0:E], r_raw[:, :, 0:E], gmx[:, :].unsqueeze(2).broadcast_to([P, G, E]), ALU.subtract).then_inc(S["g_sub"], 1)
                    wait_rank("g_exp")
                    dve.tensor_reduce(gsm[:, :], gp[:, :, 0:E], AX, ALU.add).then_inc(S["g_sum"], 1)
                    wait_rank("g_sum")
                    dve.reciprocal(grc[:, :], gsm[:, :]).then_inc(S["g_rec"], 1)
                    wait_rank("g_rec")
                    dve.tensor_tensor(gp[:, :, 0:E], gp[:, :, 0:E], grc[:, :].unsqueeze(2).broadcast_to([P, G, E]), ALU.mult).then_inc(S["g_prob"], 1)
                    wait_rank("g_prob")
                    for g in range(G):
                        pf = gp[:, g, 0:E].unsqueeze(1).broadcast_to([P, E, E])
                        pe_ = gp[:, g, 0:E].unsqueeze(2).broadcast_to([P, E, E])
                        ins = dve.tensor_tensor(cmp1[:, g, 0:E, 0:E], pf, pe_, ALU.is_ge)
                        ins2 = dve.tensor_tensor(cmp2[:, g, 0:E, 0:E], pf, pe_, ALU.is_gt)
                    ins2.then_inc(S["g_cmp"], 1)
                    wait_rank("g_cmp")
                    for g in range(G):
                        ins = dve.tensor_tensor(cmp1[:, g, 0:E, 0:E], cmp1[:, g, 0:E, 0:E], lt_mask[:, 0:E, 0:E], ALU.mult)
                        ins = dve.tensor_tensor(cmp2[:, g, 0:E, 0:E], cmp2[:, g, 0:E, 0:E], ge_mask[:, 0:E, 0:E], ALU.mult)
                    ins.then_inc(S["g_lt"], 1)
                    wait_rank("g_lt")
                    for g in range(G):
                        ins = dve.tensor_tensor(cmp1[:, g, 0:E, 0:E], cmp1[:, g, 0:E, 0:E], cmp2[:, g, 0:E, 0:E], ALU.add)
                    ins.then_inc(S["g_cnt"], 1)
                    wait_rank("g_cnt")
                    for g in range(G):
                        ins = dve.tensor_reduce(rank[:, g, 0:E], cmp1[:, g, 0:E, 0:E], AX, ALU.add)
                    ins.then_inc(S["g_rank"], 1)
                    wait_rank("g_rank")
                    dve.tensor_scalar(gsel[:, :, 0:E], rank[:, :, 0:E], 1.5, None, ALU.is_lt).then_inc(S["g_sel"], 1)
                    wait_rank("g_sel")
                    dve.tensor_tensor(gtop[:, :, 0:E], gp[:, :, 0:E], gsel[:, :, 0:E], ALU.mult).then_inc(S["g_top"], 1)
                    wait_rank("g_top")
                    dve.tensor_reduce(gsm[:, :], gtop[:, :, 0:E], AX, ALU.add).then_inc(S["g_tsum"], 1)
                    wait_rank("g_tsum")

                layer_norm(2, 2, xres, lambda g: wait("res", 2 + g // 2 + 1))
                xT_copy(2)
                wait("r_psum", 1)
                dve.tensor_copy(r_raw[:, :, 0:E0], bank[7][:, 0:G * E0].rearrange("p (g e) -> p g e", e=E0)).then_inc(S["r_fix"], 1)

                def router():
                    row_stats(3, xn, lambda g: wait("xn", 8 + g + 1))
                    refine(rstd, mv, parts, 3, "ln")
                    wait("r_fix", 1)
                    for g in range(G):
                        ins = dve.tensor_scalar(rank[:, g, 0:E0], rsum[:, 0, :], mv[:, g, 0:1], -1.0, ALU.mult, ALU.mult)
                    ins.then_inc(S["r_fix"], 1)
                    wait("r_fix", 2)
                    dve.tensor_tensor(r_raw[:, :, 0:E0], r_raw[:, :, 0:E0], rank[:, :, 0:E0], ALU.add).then_inc(S["r_fix"], 1)
                    wait("r_fix", 3)
                    for g in range(G):
                        ins = dve.scalar_tensor_tensor(out=r_lg[:, g, 0:E0], in0=r_raw[:, g, 0:E0], scalar=rstd[:, g:g + 1], in1=rsum[:, 1, :], op0=ALU.mult, op1=ALU.add)
                    ins.then_inc(S["g_cmp2"], 1)
                    wait("g_cmp2", 1)
                    dve.tensor_copy(r_raw[:, :, 0:E0], r_lg[:, :, 0:E0]).then_inc(S["g_cmp2"], 1)
                    wait("g_cmp2", 2)
                    gates(0, E0)
                    dve.tensor_scalar(gsm[:, :], gsm[:, :], 1e-8, None, ALU.add).then_inc(S["g_ge"], 1)
                    wait("g_ge", 1)
                    dve.reciprocal(grc[:, :], gsm[:, :]).then_inc(S["g_trec"], 1)
                    wait("g_trec", 1)
                    dve.tensor_tensor(gate[:, :, 0:E0], gtop[:, :, 0:E0], grc[:, :].unsqueeze(2).broadcast_to([P, G, E0]), ALU.mult).then_inc(S["g_w"], 1)
                    wait("g_w", 1)

                for e in range(E0 + 1):
                    if e < E0:
                        for g in range(G):
                            wait("up_psum", 4 * e + g + 1)
                            dve.bn_stats(ust[:, g, :], bank[g][:, :]).then_inc(S["up_stats"], 1)
                        wait("up_stats", 4 * e + 4)
                        row_moments(ust, uparts, umv, e, "up", H0)
                        refine(urs, umv, uparts, e, "up")
                        for g in range(G):
                            if e >= 2:
                                wait("zT_psum", KC0 * (e - 1))
                            dve.tensor_scalar(z[:, e % 2, g, :], bank[g][:, :], umv[:, g, 0:1], urs[:, g:g + 1], ALU.subtract, ALU.mult).then_inc(S["z"], 1)
                    if e == 1:
                        router()
                    if e > 0:
                        for g in range(G):
                            wait("dn_psum", 2 * (e - 1) + g // 2 + 1)
                            y = bank[6 + g // 2][:, (g % 2) * D:(g % 2 + 1) * D]
                            if e == 1:
                                dve.tensor_scalar(acc[:, g, :], y, gate[:, g, 0:1], None, ALU.mult).then_inc(S["acc"], 1)
                            else:
                                wait("acc", 4 * (e - 2) + g + 1)
                                dve.scalar_tensor_tensor(out=acc[:, g, :], in0=y, scalar=gate[:, g, e - 1:e], in1=acc[:, g, :], op0=ALU.mult, op1=ALU.add).then_inc(S["acc"], 1)
                row_stats(4, acc, lambda g: wait("acc", 12 + g + 1))
                refine(rstd, mv, parts, 4, "ln")
                for g in range(G):
                    dve.tensor_scalar(acc[:, g, :], acc[:, g, :], mv[:, g, 0:1], rstd[:, g:g + 1], ALU.subtract, ALU.mult).then_inc(S["moe_g"], 1)
                wait("bias_res", 3)
                for m in range(2):
                    dve.tensor_tensor(xres[:, 2 * m:2 * m + 2, :], xres[:, 2 * m:2 * m + 2, :], acc[:, 2 * m:2 * m + 2, :], ALU.add).then_inc(S["res"], 1)

                layer_norm(3, 5, xres, lambda g: wait("res", 4 + g // 2 + 1))
                xT_copy(3)
                wait("k_psum", 3)
                dve.tensor_copy(KT[:, 0, :], bank[3][:, :]).then_inc(S["k"], 1)
                for c in range(C):
                    wait("q_psum", 2 + c + 1)
                    dve.tensor_copy(QT[:, c, :], bank[4 + c][:, :]).then_inc(S["q"], 1)
                wait("v_psum", 3)
                for m in range(2):
                    for g in (2 * m, 2 * m + 1):
                        ins = dve.tensor_copy(V2[:, g, :, 0:HD], bank[2][:, g * HD:(g + 1) * HD].unsqueeze(1).broadcast_to([P, NH, HD]))
                    ins.then_inc(S["v"], 1)
                attention(1)
                add_y(1, 6)

                for c in range(C):
                    wait("k_psum", 3 + c + 1)
                    wait("km", KM_BEFORE[2])
                    dve.tensor_copy(KT[:, c, :], bank[2 + c][:, :]).then_inc(S["k"], 1)
                for m in range(2):
                    wait("v_psum", 3 + m + 1)
                    v_heads(m, False).then_inc(S["v"], 1)
                layer_norm(4, 6, xres, lambda g: wait("res", 6 + g // 2 + 1))
                xT_copy(4)
                for c in range(C):
                    wait("q_psum", 4 + c + 1)
                    dve.tensor_copy(QT[:, c, :], bank[6 + c][:, :]).then_inc(S["q"], 1)
                attention(2)
                add_y(2, 8)

                layer_norm(5, 7, xres, lambda g: wait("res", 8 + g // 2 + 1))
                xT_copy(5)
                wait("gl_psum", 1)
                dve.tensor_copy(r_raw[:, :, :], bank[6][:, 0:G * E1].rearrange("p (g e) -> p g e", e=E1)).then_inc(S["g_ge"], 1)
                wait("g_ge", 2)
                gates(1, E1)
                dve.tensor_tensor(gate[:, :, :], gsel[:, :, :], gsm[:, :].unsqueeze(2).broadcast_to([P, G, E1]), ALU.mult).then_inc(S["g_w"], 1)
                wait("gT_psum", 1)
                dve.tensor_copy(gT[:, :], bank[7][0:E1, :]).then_inc(S["gT"], 1)
                for m in range(2):
                    wait("b2_psum", m + 1)
                    dve.tensor_tensor(xres[:, 2 * m:2 * m + 2, :].rearrange("p g d -> p (g d)"), xres[:, 2 * m:2 * m + 2, :].rearrange("p g d -> p (g d)"), bank[m][:, :], ALU.add).then_inc(S["acc1"], 1)
                for e in range(E1):
                    for g in range(G):
                        n = 2 * e + g // 2
                        wait("y1_psum", n + 1)
                        wait("acc1", 2 if e == 0 else 2 + 4 * (e - 1) + g + 1)
                        ins = dve.scalar_tensor_tensor(out=xres[:, g, :], in0=bank[4 + n % 4][:, (g % 2) * D:(g % 2 + 1) * D], scalar=gate[:, g, e:e + 1], in1=xres[:, g, :], op0=ALU.mult, op1=ALU.add)
                        ins.then_inc(S["acc1"], 1)


LN_TABLE = "natural_log"
LN_EXP_TABLE = "natural_log_exp_and_others"
SPLIT = 4097.0
REF_STEPS = 837
SET_POOL = 61
SET_DVE = 15
K_BEFORE = (0, 2, 3)
KM_BEFORE = (0, 8, 12)


_OUTS = [((64, 128, 256), 'float32')]


def kernel(**inputs):
    import numpy as _np
    import concourse.bacc as _bacc
    from concourse import mybir as _mybir
    from concourse.bass_utils import run_bass_kernel_spmd as _run

    nc = _bacc.Bacc("TRN2", target_bir_lowering=False, num_devices=1)
    arrays, args = {}, {}
    for name in inputs:
        v = _np.ascontiguousarray(inputs[name])
        arrays[f"in_{name}_dram"] = v
        args[name] = nc.dram_tensor(f"in_{name}_dram", v.shape, _mybir.dt.from_np(v.dtype), kind="ExternalInput").ap()
    shape, dtype = _OUTS[0]
    out = nc.dram_tensor("out_0_dram", shape, _mybir.dt.from_np(_np.dtype(dtype)), kind="ExternalOutput").ap()
    decoder_kernel(nc, args, out)
    r = _run(nc, [arrays], core_ids=[0])
    return r.results[0]["out_0_dram"]
```
